# Optimizing a Trainium2 kernel written in Bass

```python
import numpy as np
import jax
import jax.numpy as jnp

def _softmax(x, axis=-1):
    return jax.nn.softmax(x, axis=axis)

def _gelu(x):
    return jax.nn.gelu(x, approximate=True)

def _silu(x):
    return jax.nn.silu(x)

def _sigmoid(x):
    return jax.nn.sigmoid(x)

def _layernorm(x, axis=-1, eps=1e-05):
    m = jnp.mean(x, axis=axis, keepdims=True)
    v = jnp.var(x, axis=axis, keepdims=True)
    return (x - m) / jnp.sqrt(v + eps)

def _scatter_add(tgt, idx, src, axis=0):
    return tgt.at[idx].add(src)

def _segment_sum(src, seg, n):
    return jax.ops.segment_sum(src, seg, n)
kernel_name = 'mk_xattn_seq_d4_seqx_r8_b01fb3'

def setup_inputs(seed: int=0):
    np.random.seed(seed)
    _w = jnp.asarray

    def _rec_inputs():
        import jax
        import jax.numpy as jnp
        _rk = jax.random.key(seed)
        x = -0.0003929 + 0.9999 * jax.random.normal(jax.random.fold_in(_rk, 1), (8, 256, 256), jnp.float32)
        _lenS = 256 - jax.random.randint(jax.random.fold_in(_rk, 7), (8,), 0, max(1, 256 // 4) + 1, jnp.int32)
        _lenS2 = 64 - jax.random.randint(jax.random.fold_in(_rk, 8), (8,), 0, max(1, 64 // 4) + 1, jnp.int32)
        _ctx_2048P = jax.random.normal(jax.random.fold_in(_rk, 11), (8, 16, 256), jnp.float32)
        _ctx_2048c = jax.random.dirichlet(jax.random.fold_in(_rk, 511), 0.3 * jnp.ones((16,), jnp.float32), (8, 64))
        _ctx_2048t = jnp.einsum('bsk,bkd->bsd', _ctx_2048c, _ctx_2048P)
        _ctx_2048t = _ctx_2048t * jax.lax.rsqrt(jnp.mean(jnp.square(_ctx_2048t)) + 1e-12) * 0.953939
        ctx_2048 = -8.57375e-05 + 0.999917 * (_ctx_2048t + 0.3 * jax.random.normal(jax.random.fold_in(_rk, 611), (8, 64, 256), jnp.float32))
        _validS = jnp.arange(256)[None, :] < _lenS[:, None]
        _validS2 = jnp.arange(64)[None, :] < _lenS2[:, None]
        _causal = jnp.tril(jnp.ones((256, 256), dtype=bool))
        mask_BxS2_bf1 = jnp.ones((8, 64), dtype=bool)
        mask_Bx1xSxS2_ff0 = jnp.where(jnp.ones((8, 1, 256, 64), dtype=bool), 0.0, -1000000000.0).astype(jnp.float32)
        return (x, ctx_2048, mask_BxS2_bf1, mask_Bx1xSxS2_ff0)
    x, ctx_2048, mask_BxS2_bf1, mask_Bx1xSxS2_ff0 = _rec_inputs()

    def _L0_xattn_setup():
        import jax, jax.numpy as jnp
        import numpy as np
        HIDDEN = 256
        HEADS = 16
        HEAD_DIM = HIDDEN // HEADS
        LN_EPS = 1e-05
        GATE_INIT = 0.5

        def _layer_norm(x, gamma, beta):
            mu = jnp.mean(x, axis=-1, keepdims=True)
            var = jnp.mean(jnp.square(x - mu), axis=-1, keepdims=True)
            return (x - mu) * jax.lax.rsqrt(var + LN_EPS) * gamma + beta
        key = jax.random.key(seed)
        ks = jax.random.split(key, 8)
        B, T_TEXT, T_AUDIO = (4, 256, 1500)
        s = 0.02
        return {'hidden_states': jax.random.normal(ks[0], (B, T_TEXT, HIDDEN), jnp.float32), 'audio_kv': jax.random.normal(ks[1], (B, T_AUDIO, HIDDEN), jnp.float32), 'audio_attention_mask': jnp.ones((B, T_AUDIO), dtype=bool), 'Wq': jax.random.normal(ks[2], (HIDDEN, HIDDEN), jnp.float32) * s, 'Wk': jax.random.normal(ks[3], (HIDDEN, HIDDEN), jnp.float32) * s, 'Wv': jax.random.normal(ks[4], (HIDDEN, HIDDEN), jnp.float32) * s, 'Wo': jax.random.normal(ks[5], (HIDDEN, HIDDEN), jnp.float32) * s, 'ln_gamma': jnp.ones((HIDDEN,), jnp.float32), 'ln_beta': jnp.zeros((HIDDEN,), jnp.float32), 'gate': jnp.array([GATE_INIT], jnp.float32)}
    _L0_xattn_all = _L0_xattn_setup()
    _L0_xattn_in = {k: v for k, v in _L0_xattn_all.items() if k in ('Wq', 'Wk', 'Wv', 'Wo', 'ln_gamma', 'ln_beta', 'gate')}
    del _L0_xattn_all

    def _L1_xattn_setup():
        import jax, jax.numpy as jnp
        import numpy as np
        H = 256
        NH = 32
        KVH = 8
        HD = H // NH
        GROUPS = NH // KVH
        EPS = 1e-06
        B, L, S = (4, 128, 128)

        def _gqa_forward(hidden_state, encoder_hidden_state, encoder_attention_mask, Wq, bq, Wk, bk, Wv, bv, Wo, bo, gamma, beta):
            b, l, _ = hidden_state.shape
            s = encoder_hidden_state.shape[1]
            q = hidden_state @ Wq + bq
            k = encoder_hidden_state @ Wk + bk
            v = encoder_hidden_state @ Wv + bv
            q = q.reshape(b, l, KVH, GROUPS, HD).transpose(0, 2, 3, 1, 4)
            k = k.reshape(b, s, KVH, HD).transpose(0, 2, 1, 3)
            v = v.reshape(b, s, KVH, HD).transpose(0, 2, 1, 3)
            scale = 1.0 / jnp.sqrt(jnp.asarray(HD, q.dtype))
            scores = jnp.einsum('bkgld,bksd->bkgls', q, k) * scale
            scores = scores + encoder_attention_mask[:, :, None, :, :]
            attn = jax.nn.softmax(scores, axis=-1)
            out = jnp.einsum('bkgls,bksd->bkgld', attn, v)
            out = out.transpose(0, 3, 1, 2, 4).reshape(b, l, H)
            out = out @ Wo + bo
            x = out + hidden_state
            mu = jnp.mean(x, axis=-1, keepdims=True)
            var = jnp.var(x, axis=-1, keepdims=True)
            return (x - mu) * jax.lax.rsqrt(var + EPS) * gamma + beta
        key = jax.random.key(seed)
        ks = jax.random.split(key, 12)
        sd = 0.02
        return {'hidden_state': jax.random.normal(ks[0], (B, L, H), jnp.float32), 'encoder_hidden_state': jax.random.normal(ks[1], (B, S, H), jnp.float32), 'encoder_attention_mask': jnp.zeros((B, 1, L, S), jnp.float32), 'Wq': jax.random.normal(ks[2], (H, H), jnp.float32) * sd, 'bq': jnp.zeros((H,), jnp.float32), 'Wk': jax.random.normal(ks[3], (H, KVH * HD), jnp.float32) * sd, 'bk': jnp.zeros((KVH * HD,), jnp.float32), 'Wv': jax.random.normal(ks[4], (H, KVH * HD), jnp.float32) * sd, 'bv': jnp.zeros((KVH * HD,), jnp.float32), 'Wo': jax.random.normal(ks[5], (H, H), jnp.float32) * sd, 'bo': jnp.zeros((H,), jnp.float32), 'gamma': jnp.ones((H,), jnp.float32), 'beta': jnp.zeros((H,), jnp.float32)}
    _L1_xattn_all = _L1_xattn_setup()
    _L1_xattn_in = {k: v for k, v in _L1_xattn_all.items() if k in ('Wq', 'bq', 'Wk', 'bk', 'Wv', 'bv', 'Wo', 'bo', 'gamma', 'beta')}
    del _L1_xattn_all

    def _L2_xattn_setup():
        import jax, jax.numpy as jnp
        import numpy as np
        D = 256
        H = 16
        HD = D // H
        INNER = 4 * D
        EPS = 1e-05

        def layer_norm(x, w, b):
            mu = jnp.mean(x, axis=-1, keepdims=True)
            var = jnp.mean(jnp.square(x - mu), axis=-1, keepdims=True)
            return (x - mu) * jax.lax.rsqrt(var + EPS) * w + b
        key = jax.random.key(seed)
        ks = jax.random.split(key, 12)
        B, LQ, LK = (4, 128, 256)
        std = 0.02
        inp = {'hidden_states': jax.random.normal(ks[0], (B, LQ, D), jnp.float32), 'encoder_hidden_states': jax.random.normal(ks[1], (B, LK, D), jnp.float32), 'encoder_attention_mask': jnp.ones((B, LK), dtype=bool), 'ln1_w': jnp.ones((D,), jnp.float32), 'ln1_b': jnp.zeros((D,), jnp.float32), 'q_w': jax.random.normal(ks[2], (D, D), jnp.float32) * std, 'q_b': jnp.zeros((D,), jnp.float32), 'k_w': jax.random.normal(ks[3], (D, D), jnp.float32) * std, 'k_b': jnp.zeros((D,), jnp.float32), 'v_w': jax.random.normal(ks[4], (D, D), jnp.float32) * std, 'v_b': jnp.zeros((D,), jnp.float32), 'cproj_w': jax.random.normal(ks[5], (D, D), jnp.float32) * std, 'cproj_b': jnp.zeros((D,), jnp.float32), 'ln2_w': jnp.ones((D,), jnp.float32), 'ln2_b': jnp.zeros((D,), jnp.float32), 'fc_w': jax.random.normal(ks[6], (D, INNER), jnp.float32) * std, 'fc_b': jnp.zeros((INNER,), jnp.float32), 'proj_w': jax.random.normal(ks[7], (INNER, D), jnp.float32) * std, 'proj_b': jnp.zeros((D,), jnp.float32)}
        return inp
    _L2_xattn_all = _L2_xattn_setup()
    _L2_xattn_in = {k: v for k, v in _L2_xattn_all.items() if k in ('ln1_w', 'ln1_b', 'q_w', 'q_b', 'k_w', 'k_b', 'v_w', 'v_b', 'cproj_w', 'cproj_b', 'ln2_w', 'ln2_b', 'fc_w', 'fc_b', 'proj_w', 'proj_b')}
    del _L2_xattn_all

    def _L3_xattn_setup():
        import jax, jax.numpy as jnp
        import numpy as np
        B, Q, S1, S2 = (4, 32, 256, 256)
        D, H, K, F = (256, 16, 128, 1024)
        LN_EPS = 1e-05

        def _layer_norm(x, scale, offset):
            mu = jnp.mean(x, axis=-1, keepdims=True)
            var = jnp.var(x, axis=-1, keepdims=True)
            return (x - mu) * jax.lax.rsqrt(var + LN_EPS) * scale + offset

        def _cross_attention(q_in, kv_in, wq, bq, wk, bk, wv, bv, wo, bo, bias_k, bias_v):
            b, q_len, _ = q_in.shape
            t = kv_in.shape[1]
            qh = (q_in @ wq + bq).reshape(b, q_len, H, K)
            kh = (kv_in @ wk + bk).reshape(b, t, H, K)
            vh = (kv_in @ wv + bv).reshape(b, t, H, K)
            kh = jnp.concatenate([kh, jnp.broadcast_to(bias_k, (b, 1, H, K))], axis=1)
            vh = jnp.concatenate([vh, jnp.broadcast_to(bias_v, (b, 1, H, K))], axis=1)
            scale = jnp.sqrt(jnp.asarray(K, q_in.dtype))
            logits = jnp.einsum('bqhk,bthk->bhqt', qh, kh) / scale
            weights = jax.nn.softmax(logits, axis=-1)
            ctx = jnp.einsum('bhqt,bthk->bqhk', weights, vh).reshape(b, q_len, H * K)
            return ctx @ wo + bo

        def _forward(x, xf_1, xf_2, ln1_scale, ln1_offset, wq1, bq1, wk1, bk1, wv1, bv1, wo1, bo1, bias_k1, bias_v1, ln2_scale, ln2_offset, wq2, bq2, wk2, bk2, wv2, bv2, wo2, bo2, bias_k2, bias_v2, ln_mlp_scale, ln_mlp_offset, w_fc1, b_fc1, w_fc2, b_fc2):
            res = x
            h = _layer_norm(x, ln1_scale, ln1_offset)
            x = res + _cross_attention(h, xf_1, wq1, bq1, wk1, bk1, wv1, bv1, wo1, bo1, bias_k1, bias_v1)
            res = x
            h = _layer_norm(x, ln2_scale, ln2_offset)
            x = res + _cross_attention(h, xf_2, wq2, bq2, wk2, bk2, wv2, bv2, wo2, bo2, bias_k2, bias_v2)
            h = _layer_norm(x, ln_mlp_scale, ln_mlp_offset)
            h = jax.nn.gelu(h @ w_fc1 + b_fc1, approximate=False) @ w_fc2 + b_fc2
            return x + h
        key = jax.random.key(seed)
        ks = iter(jax.random.split(key, 64))

        def rn(shape, s=0.02):
            return jax.random.normal(next(ks), shape, jnp.float32) * s
        inp = {'x': rn((B, Q, D), 1.0), 'xf_1': rn((B, S1, D), 1.0), 'xf_2': rn((B, S2, D), 1.0)}
        for i in (1, 2):
            inp[f'ln{i}_scale'] = jnp.ones((D,), jnp.float32)
            inp[f'ln{i}_offset'] = jnp.zeros((D,), jnp.float32)
            inp[f'wq{i}'] = rn((D, H * K))
            inp[f'bq{i}'] = jnp.zeros((H * K,), jnp.float32)
            inp[f'wk{i}'] = rn((D, H * K))
            inp[f'bk{i}'] = jnp.zeros((H * K,), jnp.float32)
            inp[f'wv{i}'] = rn((D, H * K))
            inp[f'bv{i}'] = jnp.zeros((H * K,), jnp.float32)
            inp[f'wo{i}'] = rn((H * K, D))
            inp[f'bo{i}'] = jnp.zeros((D,), jnp.float32)
            inp[f'bias_k{i}'] = rn((1, 1, H, K))
            inp[f'bias_v{i}'] = rn((1, 1, H, K))
        inp['ln_mlp_scale'] = jnp.ones((D,), jnp.float32)
        inp['ln_mlp_offset'] = jnp.zeros((D,), jnp.float32)
        inp['w_fc1'] = rn((D, F))
        inp['b_fc1'] = jnp.zeros((F,), jnp.float32)
        inp['w_fc2'] = rn((F, D))
        inp['b_fc2'] = jnp.zeros((D,), jnp.float32)
        return inp
    _L3_xattn_all = _L3_xattn_setup()
    _L3_xattn_in = {k: v for k, v in _L3_xattn_all.items() if k in ('ln1_scale', 'ln1_offset', 'wq1', 'bq1', 'wk1', 'bk1', 'wv1', 'bv1', 'wo1', 'bo1', 'bias_k1', 'bias_v1', 'ln2_scale', 'ln2_offset', 'wq2', 'bq2', 'wk2', 'bk2', 'wv2', 'bv2', 'wo2', 'bo2', 'bias_k2', 'bias_v2', 'ln_mlp_scale', 'ln_mlp_offset', 'w_fc1', 'b_fc1', 'w_fc2', 'b_fc2')}
    del _L3_xattn_all
    return {'x': x, 'ctx_2048': ctx_2048, 'mask_BxS2_bf1': mask_BxS2_bf1, 'mask_Bx1xSxS2_ff0': mask_Bx1xSxS2_ff0, 'L0_xattn_Wq': _L0_xattn_in['Wq'], 'L0_xattn_Wk': _L0_xattn_in['Wk'], 'L0_xattn_Wv': _L0_xattn_in['Wv'], 'L0_xattn_Wo': _L0_xattn_in['Wo'], 'L0_xattn_ln_gamma': _L0_xattn_in['ln_gamma'], 'L0_xattn_ln_beta': _L0_xattn_in['ln_beta'], 'L0_xattn_gate': _L0_xattn_in['gate'], 'L1_xattn_Wq': _L1_xattn_in['Wq'], 'L1_xattn_bq': _L1_xattn_in['bq'], 'L1_xattn_Wk': _L1_xattn_in['Wk'], 'L1_xattn_bk': _L1_xattn_in['bk'], 'L1_xattn_Wv': _L1_xattn_in['Wv'], 'L1_xattn_bv': _L1_xattn_in['bv'], 'L1_xattn_Wo': _L1_xattn_in['Wo'], 'L1_xattn_bo': _L1_xattn_in['bo'], 'L1_xattn_gamma': _L1_xattn_in['gamma'], 'L1_xattn_beta': _L1_xattn_in['beta'], 'L2_xattn_ln1_w': _L2_xattn_in['ln1_w'], 'L2_xattn_ln1_b': _L2_xattn_in['ln1_b'], 'L2_xattn_q_w': _L2_xattn_in['q_w'], 'L2_xattn_q_b': _L2_xattn_in['q_b'], 'L2_xattn_k_w': _L2_xattn_in['k_w'], 'L2_xattn_k_b': _L2_xattn_in['k_b'], 'L2_xattn_v_w': _L2_xattn_in['v_w'], 'L2_xattn_v_b': _L2_xattn_in['v_b'], 'L2_xattn_cproj_w': _L2_xattn_in['cproj_w'], 'L2_xattn_cproj_b': _L2_xattn_in['cproj_b'], 'L2_xattn_ln2_w': _L2_xattn_in['ln2_w'], 'L2_xattn_ln2_b': _L2_xattn_in['ln2_b'], 'L2_xattn_fc_w': _L2_xattn_in['fc_w'], 'L2_xattn_fc_b': _L2_xattn_in['fc_b'], 'L2_xattn_proj_w': _L2_xattn_in['proj_w'], 'L2_xattn_proj_b': _L2_xattn_in['proj_b'], 'L3_xattn_ln1_scale': _L3_xattn_in['ln1_scale'], 'L3_xattn_ln1_offset': _L3_xattn_in['ln1_offset'], 'L3_xattn_wq1': _L3_xattn_in['wq1'], 'L3_xattn_bq1': _L3_xattn_in['bq1'], 'L3_xattn_wk1': _L3_xattn_in['wk1'], 'L3_xattn_bk1': _L3_xattn_in['bk1'], 'L3_xattn_wv1': _L3_xattn_in['wv1'], 'L3_xattn_bv1': _L3_xattn_in['bv1'], 'L3_xattn_wo1': _L3_xattn_in['wo1'], 'L3_xattn_bo1': _L3_xattn_in['bo1'], 'L3_xattn_bias_k1': _L3_xattn_in['bias_k1'], 'L3_xattn_bias_v1': _L3_xattn_in['bias_v1'], 'L3_xattn_ln2_scale': _L3_xattn_in['ln2_scale'], 'L3_xattn_ln2_offset': _L3_xattn_in['ln2_offset'], 'L3_xattn_wq2': _L3_xattn_in['wq2'], 'L3_xattn_bq2': _L3_xattn_in['bq2'], 'L3_xattn_wk2': _L3_xattn_in['wk2'], 'L3_xattn_bk2': _L3_xattn_in['bk2'], 'L3_xattn_wv2': _L3_xattn_in['wv2'], 'L3_xattn_bv2': _L3_xattn_in['bv2'], 'L3_xattn_wo2': _L3_xattn_in['wo2'], 'L3_xattn_bo2': _L3_xattn_in['bo2'], 'L3_xattn_bias_k2': _L3_xattn_in['bias_k2'], 'L3_xattn_bias_v2': _L3_xattn_in['bias_v2'], 'L3_xattn_ln_mlp_scale': _L3_xattn_in['ln_mlp_scale'], 'L3_xattn_ln_mlp_offset': _L3_xattn_in['ln_mlp_offset'], 'L3_xattn_w_fc1': _L3_xattn_in['w_fc1'], 'L3_xattn_b_fc1': _L3_xattn_in['b_fc1'], 'L3_xattn_w_fc2': _L3_xattn_in['w_fc2'], 'L3_xattn_b_fc2': _L3_xattn_in['b_fc2']}

def reference(x, ctx_2048, mask_BxS2_bf1, mask_Bx1xSxS2_ff0, L0_xattn_Wq, L0_xattn_Wk, L0_xattn_Wv, L0_xattn_Wo, L0_xattn_ln_gamma, L0_xattn_ln_beta, L0_xattn_gate, L1_xattn_Wq, L1_xattn_bq, L1_xattn_Wk, L1_xattn_bk, L1_xattn_Wv, L1_xattn_bv, L1_xattn_Wo, L1_xattn_bo, L1_xattn_gamma, L1_xattn_beta, L2_xattn_ln1_w, L2_xattn_ln1_b, L2_xattn_q_w, L2_xattn_q_b, L2_xattn_k_w, L2_xattn_k_b, L2_xattn_v_w, L2_xattn_v_b, L2_xattn_cproj_w, L2_xattn_cproj_b, L2_xattn_ln2_w, L2_xattn_ln2_b, L2_xattn_fc_w, L2_xattn_fc_b, L2_xattn_proj_w, L2_xattn_proj_b, L3_xattn_ln1_scale, L3_xattn_ln1_offset, L3_xattn_wq1, L3_xattn_bq1, L3_xattn_wk1, L3_xattn_bk1, L3_xattn_wv1, L3_xattn_bv1, L3_xattn_wo1, L3_xattn_bo1, L3_xattn_bias_k1, L3_xattn_bias_v1, L3_xattn_ln2_scale, L3_xattn_ln2_offset, L3_xattn_wq2, L3_xattn_bq2, L3_xattn_wk2, L3_xattn_bk2, L3_xattn_wv2, L3_xattn_bv2, L3_xattn_wo2, L3_xattn_bo2, L3_xattn_bias_k2, L3_xattn_bias_v2, L3_xattn_ln_mlp_scale, L3_xattn_ln_mlp_offset, L3_xattn_w_fc1, L3_xattn_b_fc1, L3_xattn_w_fc2, L3_xattn_b_fc2):
    import jax
    import jax.numpy as jnp

    def _L0_xattn_ref(hidden_states, audio_kv, audio_attention_mask, Wq, Wk, Wv, Wo, ln_gamma, ln_beta, gate):
        import jax, jax.numpy as jnp
        import numpy as np
        HIDDEN = 256
        HEADS = 16
        HEAD_DIM = HIDDEN // HEADS
        LN_EPS = 1e-05
        GATE_INIT = 0.5

        def _layer_norm(x, gamma, beta):
            mu = jnp.mean(x, axis=-1, keepdims=True)
            var = jnp.mean(jnp.square(x - mu), axis=-1, keepdims=True)
            return (x - mu) * jax.lax.rsqrt(var + LN_EPS) * gamma + beta
        B, Tt, D = hidden_states.shape
        Ta = audio_kv.shape[1]
        scale = HEAD_DIM ** (-0.5)
        a = _layer_norm(audio_kv, ln_gamma, ln_beta)
        Q = (hidden_states @ Wq.T).reshape(B, Tt, HEADS, HEAD_DIM).transpose(0, 2, 1, 3)
        K = (a @ Wk.T).reshape(B, Ta, HEADS, HEAD_DIM).transpose(0, 2, 1, 3)
        V = (a @ Wv.T).reshape(B, Ta, HEADS, HEAD_DIM).transpose(0, 2, 1, 3)
        scores = jnp.einsum('bhtd,bhsd->bhts', Q, K) * scale
        mask = audio_attention_mask[:, None, None, :]
        scores = jnp.where(mask, scores, jnp.float32(-jnp.inf))
        attn = jax.nn.softmax(scores, axis=-1)
        out = jnp.einsum('bhts,bhsd->bhtd', attn, V)
        out = out.transpose(0, 2, 1, 3).reshape(B, Tt, D)
        out = out @ Wo.T
        return hidden_states + jnp.tanh(gate) * out

    def _L1_xattn_ref(hidden_state, encoder_hidden_state, encoder_attention_mask, Wq, bq, Wk, bk, Wv, bv, Wo, bo, gamma, beta):
        import jax, jax.numpy as jnp
        import numpy as np
        H = 256
        NH = 32
        KVH = 8
        HD = H // NH
        GROUPS = NH // KVH
        EPS = 1e-06
        B, L, S = (4, 128, 128)

        def _gqa_forward(hidden_state, encoder_hidden_state, encoder_attention_mask, Wq, bq, Wk, bk, Wv, bv, Wo, bo, gamma, beta):
            b, l, _ = hidden_state.shape
            s = encoder_hidden_state.shape[1]
            q = hidden_state @ Wq + bq
            k = encoder_hidden_state @ Wk + bk
            v = encoder_hidden_state @ Wv + bv
            q = q.reshape(b, l, KVH, GROUPS, HD).transpose(0, 2, 3, 1, 4)
            k = k.reshape(b, s, KVH, HD).transpose(0, 2, 1, 3)
            v = v.reshape(b, s, KVH, HD).transpose(0, 2, 1, 3)
            scale = 1.0 / jnp.sqrt(jnp.asarray(HD, q.dtype))
            scores = jnp.einsum('bkgld,bksd->bkgls', q, k) * scale
            scores = scores + encoder_attention_mask[:, :, None, :, :]
            attn = jax.nn.softmax(scores, axis=-1)
            out = jnp.einsum('bkgls,bksd->bkgld', attn, v)
            out = out.transpose(0, 3, 1, 2, 4).reshape(b, l, H)
            out = out @ Wo + bo
            x = out + hidden_state
            mu = jnp.mean(x, axis=-1, keepdims=True)
            var = jnp.var(x, axis=-1, keepdims=True)
            return (x - mu) * jax.lax.rsqrt(var + EPS) * gamma + beta
        return _gqa_forward(hidden_state, encoder_hidden_state, encoder_attention_mask, Wq, bq, Wk, bk, Wv, bv, Wo, bo, gamma, beta)

    def _L2_xattn_ref(hidden_states, encoder_hidden_states, encoder_attention_mask, ln1_w, ln1_b, q_w, q_b, k_w, k_b, v_w, v_b, cproj_w, cproj_b, ln2_w, ln2_b, fc_w, fc_b, proj_w, proj_b):
        import jax, jax.numpy as jnp
        import numpy as np
        D = 256
        H = 16
        HD = D // H
        INNER = 4 * D
        EPS = 1e-05

        def layer_norm(x, w, b):
            mu = jnp.mean(x, axis=-1, keepdims=True)
            var = jnp.mean(jnp.square(x - mu), axis=-1, keepdims=True)
            return (x - mu) * jax.lax.rsqrt(var + EPS) * w + b
        B, LQ, _ = hidden_states.shape
        LK = encoder_hidden_states.shape[1]
        residual = hidden_states
        x = layer_norm(hidden_states, ln1_w, ln1_b)
        q = (x @ q_w + q_b).reshape(B, LQ, H, HD).transpose(0, 2, 1, 3)
        k = (encoder_hidden_states @ k_w + k_b).reshape(B, LK, H, HD).transpose(0, 2, 1, 3)
        v = (encoder_hidden_states @ v_w + v_b).reshape(B, LK, H, HD).transpose(0, 2, 1, 3)
        scale = 1.0 / np.sqrt(HD).astype(np.float32)
        scores = jnp.einsum('bhqd,bhkd->bhqk', q, k) * scale
        mask = encoder_attention_mask[:, None, None, :]
        mask_value = jnp.finfo(scores.dtype).min
        scores = jnp.where(mask, scores, mask_value)
        attn = jax.nn.softmax(scores, axis=-1)
        out = jnp.einsum('bhqk,bhkd->bhqd', attn, v)
        out = out.transpose(0, 2, 1, 3).reshape(B, LQ, D)
        out = out @ cproj_w + cproj_b
        hidden = out + residual
        residual = hidden
        y = layer_norm(hidden, ln2_w, ln2_b)
        y = jax.nn.gelu(y @ fc_w + fc_b, approximate=True)
        y = y @ proj_w + proj_b
        return residual + y

    def _L3_xattn_ref(x, xf_1, xf_2, ln1_scale, ln1_offset, wq1, bq1, wk1, bk1, wv1, bv1, wo1, bo1, bias_k1, bias_v1, ln2_scale, ln2_offset, wq2, bq2, wk2, bk2, wv2, bv2, wo2, bo2, bias_k2, bias_v2, ln_mlp_scale, ln_mlp_offset, w_fc1, b_fc1, w_fc2, b_fc2):
        import jax, jax.numpy as jnp
        import numpy as np
        B, Q, S1, S2 = (4, 32, 256, 256)
        D, H, K, F = (256, 16, 128, 1024)
        LN_EPS = 1e-05

        def _layer_norm(x, scale, offset):
            mu = jnp.mean(x, axis=-1, keepdims=True)
            var = jnp.var(x, axis=-1, keepdims=True)
            return (x - mu) * jax.lax.rsqrt(var + LN_EPS) * scale + offset

        def _cross_attention(q_in, kv_in, wq, bq, wk, bk, wv, bv, wo, bo, bias_k, bias_v):
            b, q_len, _ = q_in.shape
            t = kv_in.shape[1]
            qh = (q_in @ wq + bq).reshape(b, q_len, H, K)
            kh = (kv_in @ wk + bk).reshape(b, t, H, K)
            vh = (kv_in @ wv + bv).reshape(b, t, H, K)
            kh = jnp.concatenate([kh, jnp.broadcast_to(bias_k, (b, 1, H, K))], axis=1)
            vh = jnp.concatenate([vh, jnp.broadcast_to(bias_v, (b, 1, H, K))], axis=1)
            scale = jnp.sqrt(jnp.asarray(K, q_in.dtype))
            logits = jnp.einsum('bqhk,bthk->bhqt', qh, kh) / scale
            weights = jax.nn.softmax(logits, axis=-1)
            ctx = jnp.einsum('bhqt,bthk->bqhk', weights, vh).reshape(b, q_len, H * K)
            return ctx @ wo + bo

        def _forward(x, xf_1, xf_2, ln1_scale, ln1_offset, wq1, bq1, wk1, bk1, wv1, bv1, wo1, bo1, bias_k1, bias_v1, ln2_scale, ln2_offset, wq2, bq2, wk2, bk2, wv2, bv2, wo2, bo2, bias_k2, bias_v2, ln_mlp_scale, ln_mlp_offset, w_fc1, b_fc1, w_fc2, b_fc2):
            res = x
            h = _layer_norm(x, ln1_scale, ln1_offset)
            x = res + _cross_attention(h, xf_1, wq1, bq1, wk1, bk1, wv1, bv1, wo1, bo1, bias_k1, bias_v1)
            res = x
            h = _layer_norm(x, ln2_scale, ln2_offset)
            x = res + _cross_attention(h, xf_2, wq2, bq2, wk2, bk2, wv2, bv2, wo2, bo2, bias_k2, bias_v2)
            h = _layer_norm(x, ln_mlp_scale, ln_mlp_offset)
            h = jax.nn.gelu(h @ w_fc1 + b_fc1, approximate=False) @ w_fc2 + b_fc2
            return x + h
        return _forward(x, xf_1, xf_2, ln1_scale, ln1_offset, wq1, bq1, wk1, bk1, wv1, bv1, wo1, bo1, bias_k1, bias_v1, ln2_scale, ln2_offset, wq2, bq2, wk2, bk2, wv2, bv2, wo2, bo2, bias_k2, bias_v2, ln_mlp_scale, ln_mlp_offset, w_fc1, b_fc1, w_fc2, b_fc2)
    x = _L0_xattn_ref(x, ctx_2048, mask_BxS2_bf1, L0_xattn_Wq, L0_xattn_Wk, L0_xattn_Wv, L0_xattn_Wo, L0_xattn_ln_gamma, L0_xattn_ln_beta, L0_xattn_gate)
    x = _L1_xattn_ref(x, ctx_2048, mask_Bx1xSxS2_ff0, L1_xattn_Wq, L1_xattn_bq, L1_xattn_Wk, L1_xattn_bk, L1_xattn_Wv, L1_xattn_bv, L1_xattn_Wo, L1_xattn_bo, L1_xattn_gamma, L1_xattn_beta)
    x = _L2_xattn_ref(x, ctx_2048, mask_BxS2_bf1, L2_xattn_ln1_w, L2_xattn_ln1_b, L2_xattn_q_w, L2_xattn_q_b, L2_xattn_k_w, L2_xattn_k_b, L2_xattn_v_w, L2_xattn_v_b, L2_xattn_cproj_w, L2_xattn_cproj_b, L2_xattn_ln2_w, L2_xattn_ln2_b, L2_xattn_fc_w, L2_xattn_fc_b, L2_xattn_proj_w, L2_xattn_proj_b)
    x = _L3_xattn_ref(x, ctx_2048, ctx_2048, L3_xattn_ln1_scale, L3_xattn_ln1_offset, L3_xattn_wq1, L3_xattn_bq1, L3_xattn_wk1, L3_xattn_bk1, L3_xattn_wv1, L3_xattn_bv1, L3_xattn_wo1, L3_xattn_bo1, L3_xattn_bias_k1, L3_xattn_bias_v1, L3_xattn_ln2_scale, L3_xattn_ln2_offset, L3_xattn_wq2, L3_xattn_bq2, L3_xattn_wk2, L3_xattn_bk2, L3_xattn_wv2, L3_xattn_bv2, L3_xattn_wo2, L3_xattn_bo2, L3_xattn_bias_k2, L3_xattn_bias_v2, L3_xattn_ln_mlp_scale, L3_xattn_ln_mlp_offset, L3_xattn_w_fc1, L3_xattn_b_fc1, L3_xattn_w_fc2, L3_xattn_b_fc2)
    return x

_drawn_inputs = setup_inputs


def setup_inputs(seed=0):
    import zlib

    import numpy as np

    out = dict(_drawn_inputs(seed))
    spreads = {'L0_xattn_ln_gamma': (1.0, 0.6),
     'L0_xattn_ln_beta': (0.0, 0.8),
     'L1_xattn_bq': (0.0, 0.8),
     'L1_xattn_bk': (0.0, 2.0),
     'L1_xattn_bv': (0.0, 0.1),
     'L1_xattn_bo': (0.0, 0.1),
     'L1_xattn_gamma': (1.0, 0.2),
     'L1_xattn_beta': (0.0, 0.1),
     'L2_xattn_ln1_w': (1.0, 0.6),
     'L2_xattn_ln1_b': (0.0, 0.8),
     'L2_xattn_q_b': (0.0, 0.8),
     'L2_xattn_k_b': (0.0, 2.0),
     'L2_xattn_v_b': (0.0, 0.272),
     'L2_xattn_cproj_b': (0.0, 0.1),
     'L2_xattn_ln2_w': (1.0, 0.6),
     'L2_xattn_ln2_b': (0.0, 0.755),
     'L2_xattn_fc_b': (0.0, 0.1),
     'L2_xattn_proj_b': (0.0, 0.1),
     'L3_xattn_ln1_scale': (1.0, 0.6),
     'L3_xattn_ln1_offset': (0.0, 0.8),
     'L3_xattn_bq1': (0.0, 0.8),
     'L3_xattn_bk1': (0.0, 2.0),
     'L3_xattn_bv1': (0.0, 0.1),
     'L3_xattn_bo1': (0.0, 0.1),
     'L3_xattn_ln2_scale': (1.0, 0.6),
     'L3_xattn_ln2_offset': (0.0, 0.8),
     'L3_xattn_bq2': (0.0, 0.8),
     'L3_xattn_bk2': (0.0, 2.0),
     'L3_xattn_bv2': (0.0, 0.1),
     'L3_xattn_bo2': (0.0, 0.1),
     'L3_xattn_ln_mlp_scale': (1.0, 0.6),
     'L3_xattn_ln_mlp_offset': (0.0, 0.8),
     'L3_xattn_b_fc1': (0.0, 0.271),
     'L3_xattn_b_fc2': (0.0, 0.1)}
    factors = {'L0_xattn_Wq': 8.0,
     'L0_xattn_Wk': 8.0,
     'L1_xattn_Wq': 8.0,
     'L1_xattn_Wk': 8.0,
     'L2_xattn_q_w': 8.0,
     'L2_xattn_k_w': 8.0,
     'L3_xattn_wq1': 8.0,
     'L3_xattn_wk1': 8.0,
     'L3_xattn_bias_k1': 64.0,
     'L3_xattn_bias_v1': 64.0,
     'L3_xattn_wq2': 8.0,
     'L3_xattn_wk2': 8.0,
     'L3_xattn_bias_k2': 64.0,
     'L3_xattn_bias_v2': 64.0}
    for name, (base, spread) in spreads.items():
        noise = np.random.default_rng([zlib.crc32(name.encode()), seed]).standard_normal(out[name].shape)
        drawn = base * np.exp(spread * noise) if base else spread * noise
        out[name] = jnp.asarray(drawn.astype(out[name].dtype))
    for name, factor in factors.items():
        out[name] = (out[name] * factor).astype(out[name].dtype)
    return out
```

```python
from contextlib import ExitStack
from functools import partial as step

import concourse.bass as bass
from concourse import mybir

F32 = mybir.dt.float32
BF16 = mybir.dt.bfloat16
U8 = mybir.dt.uint8
ALU = mybir.AluOpType
ACT = mybir.ActivationFunctionType
X = mybir.AxisListType.X

P = 128
D = 256
DC = D // P
B, T, S = 8, 256, 64
TT = T // P
CTX = B * S
H3, K3 = 16, 128
F = 4 * D
FC = F // P
GS = 1024
GH = GS // S
BANK = 512

COLS = {"l0_g": 2, "l0_b": 2, "gate": 1, "l1_bq": 2, "l1_bk": 2, "l2_g1": 2, "l2_b1": 2, "l2_bq": 2,
        "l2_bk": 2, "l2_g2": 2, "l2_b2": 2, "l2_fcb": FC, "l3_gm": 2, "l3_bm": 2, "l3_fcb": FC}
for _a in "12":
    COLS |= {f"l3_g{_a}": 2, f"l3_b{_a}": 2, f"l3_bq{_a}": H3, f"l3_bk{_a}": H3, f"l3_bv{_a}": H3,
             f"l3_kb{_a}": H3, f"l3_vb{_a}": H3}
COL_AT, _n = {}, 0
for _k, _v in COLS.items():
    COL_AT[_k] = _n
    _n += _v
N_COLS = _n
ROWS = ["l1_bv", "l1_bo", "l1_g", "l1_b", "l2_bv", "l2_bo", "l2_pb", "l3_bo1", "l3_bo2", "l3_pb"]
ROWS_EARLY = 6


class Engine:

    def __init__(self, name, sem):
        self.name, self.sem, self.count, self.todo, self.seen = name, sem, 0, [], {}

    def wait(self, tokens):
        for sem, value in tokens:
            if self.seen.get(sem.name, 0) < value:
                self.seen[sem.name] = value
                self.todo.append(lambda e, s=sem, v=value: e.wait_ge(s, v))

    def do(self, what, *after):
        self.wait(after)
        self.count += 1
        self.todo.append(lambda e: what().then_inc(self.sem, 1))
        return self.sem, self.count

    def run(self, parts, *after):
        self.wait(after)
        self.todo.extend([lambda e, w=w: w() for w in parts[:-1]])
        return self.do(parts[-1])

    def now(self):
        return self.sem, self.count

    def emit(self, e):
        for step in self.todo:
            step(e)


class Ring:

    def __init__(self, bufs, free=()):
        self.bufs, self.free, self.order = list(bufs), [list(free) for _ in bufs], list(range(len(bufs)))

    def take(self):
        assert self.order, "every buffer is held"
        i = self.order.pop(0)
        return self.bufs[i], self.free[i], i

    def release(self, i, *tokens):
        self.free[i] = list(tokens)
        self.order.append(i)


def interleave(streams, width):
    waiting, live = list(streams), []
    while waiting or live:
        while waiting and len(live) < width:
            live.append(waiting.pop(0))
        for g in list(live):
            if next(g, "end") == "end":
                live.remove(g)


def beside(main, side, width, ratio):
    due = 0.0

    def step_side():
        nonlocal due
        due += ratio
        while due >= 1:
            due -= 1
            next(side, None)

    waiting, live = list(main), []
    while waiting or live:
        while waiting and len(live) < width:
            live.append(waiting.pop(0))
        for g in list(live):
            if next(g, "end") == "end":
                live.remove(g)
            step_side()
    for _ in side:
        pass


def build(nc, A, out):
    ctx = ExitStack()
    with ctx:
        def sb(name, shape, dt=F32):
            return ctx.enter_context(nc.sbuf_tensor(name, shape, dt))

        def sem(name):
            return ctx.enter_context(nc.semaphore(name))

        score_ring = Ring([ctx.enter_context(nc.psum_tensor(f"scores{i}", [P, GS], F32)) for i in range(2)])
        work = Ring([ctx.enter_context(nc.psum_tensor(f"work{i}", [P, BANK], F32)) for i in range(4)])

        x = sb("x", [P, B * TT, D])
        ctxT = sb("ctxT", [P, DC, CTX])
        cols = sb("cols", [P, N_COLS])
        rows_late = sb("rows_late", [P, len(ROWS) - ROWS_EARLY, D])
        ident = sb("ident", [P, P])
        ones = sb("ones", [P, P])
        minus_half = sb("minus_half", [P, CTX // P])
        ones_row = sb("ones_row", [1, P], BF16)
        tanh_gate = sb("tanh_gate", [P, 1])
        probs_bufs = [sb(f"probs{i}", [P, GS + H3])[:, :] for i in range(2)]
        probsT_bufs = [sb(f"probsT{i}", [P, GH // 2 + 1, P])[:, :, :] for i in range(2)]
        stat = Ring([sb(f"stat{i}", [P, 64]) for i in range(6)])
        kvT = Ring([sb(f"kvT{i}", [P, 4, P]) for i in range(3)])
        w3 = sb("w3", [P, 4 * H3 * D])
        PAIR = 2 * (DC * GS + GH // 2 * D + GS)
        pair = [sb(f"pair{i}", [P, PAIR]) for i in range(2)]
        act_bufs = sb("act_bufs", [P, 4, DC * T])
        vob = sb("vob", [H3, D])
        kbias = sb("kbias", [P, DC, H3])
        cbias = sb("cbias", [P, H3])

        def carve(region):
            at = 0

            def cut(*shape):
                nonlocal at
                n = 1
                for s in shape:
                    n *= s
                assert at + n <= region.shape[1], "region full"
                v, at = region[:, at:at + n], at + n
                names = "abcd"[:len(shape)]
                if len(shape) == 1:
                    return v
                return v.rearrange(f"p ({' '.join(names)}) -> p {' '.join(names)}",
                                   **{k: s for k, s in zip(names, shape)})
            return cut

        cut = carve(w3)
        w_small = {f"l{i}_w{k}": cut(DC, D) for i in range(3) for k in "qkvo"}
        kT_small = [cut(DC, CTX) for _ in range(3)]
        kdiag = Ring([cut(DC, GS) for _ in range(3)])
        cut = carve(pair[0])
        ctx_raw, ctx_norm = cut(CTX // P, D), cut(CTX // P, D)
        aT = cut(DC, CTX)
        mask_tok = cut(B * TT, S)
        rows_early = cut(ROWS_EARLY, D)
        vdiag = {16: Ring([cut(8, 34) for _ in range(3)]), 8: Ring([cut(16, 18) for _ in range(3)])}
        qT_ring = Ring([cut(DC, T) for _ in range(3)])
        oT_ring = Ring([cut(DC, T) for _ in range(2)])
        head_of_row = {16: cut(8), 8: cut(16)}
        cut = carve(pair[1])
        w_mlp = {"l2": (cut(DC, F), cut(FC, D))}
        more = [cut(DC, T) for _ in range(2)]
        hid_and_probs = cut(2 * FC * T)
        cut = carve(hid_and_probs)
        probs3, probsT3 = cut(GS + H3), cut(GH // 2 + 1, P)
        o_ring = Ring([cut(DC, T) for _ in range(3)])
        cut = carve(hid_and_probs)
        hid_bufs = [cut(FC, T) for _ in range(2)]
        probs, probsT = Ring([*probs_bufs, probs3]), Ring([*probsT_bufs, probsT3])
        fixed = [act_bufs[:, i, :].rearrange("p (c t) -> p c t", c=DC) for i in range(4)]
        srcT_ring = Ring([fixed[0], fixed[1], more[0]])
        norm_ring = Ring([fixed[2], fixed[3], more[1]])
        mask_u8 = sb("mask_u8", [1, CTX], U8)
        mask_row = {"l0": sb("mask_inf", [1, CTX], BF16), "l2": sb("mask_min", [1, CTX], BF16)}

        pe, dve, act, pool = (Engine(n, sem(f"s_{n}")) for n in ("pe", "dve", "act", "pool"))
        sp = Engine("sp", None)
        engines = (pe, dve, act, pool)

        def so_far():
            return [e.now() for e in engines]

        loads = {}

        def load(name, dst, src, *after):
            loads[name] = (sem(f"in_{name}"), 16)
            sp.wait(after)
            sp.todo.append(lambda e, s=loads[name][0]: e.dma_start(dst, src).then_inc(s, 16))
            return loads[name]

        def col(name, i=0, n=1):
            return cols[:, COL_AT[name] + i:COL_AT[name] + i + n]

        def row(name):
            i = ROWS.index(name)
            return rows_early[:, i, :] if i < ROWS_EARLY else rows_late[:, i - ROWS_EARLY, :]

        load("ctx", ctx_raw, A["ctx"].rearrange("(n p) d -> p n d", p=P))
        load("ident", ident[:, :], A["ident"])
        load("cols", cols[:, :], A["cols"])
        load("maskhead", head_of_row[16], A["head16"])
        load("maskhead8", head_of_row[8], A["head8"])
        x_tiles = A["x"].rearrange("(n p) d -> p n d", p=P)
        for k in "kvqo":
            load(f"l0_w{k}", w_small[f"l0_w{k}"], A[f"l0_w{k}"])
            if k == "k":
                load("mask", mask_u8[:, :], A["mask"])
                load("x0", x[:, 0:4, :], x_tiles[:, 0:4, :])
        load("x1", x[:, 4:16, :], x_tiles[:, 4:16, :])
        load("rows_early", rows_early, A["rows"][0:ROWS_EARLY, :].unsqueeze(0).broadcast_to([P, ROWS_EARLY, D]))
        load("rows_late", rows_late[:, :, :],
             A["rows"][ROWS_EARLY:, :].unsqueeze(0).broadcast_to([P, len(ROWS) - ROWS_EARLY, D]))
        load("mask_tok", mask_tok, A["mask_tok"].rearrange("(n p) s -> p n s", p=P))
        for i in (1, 2):
            for k in "kvqo":
                load(f"l{i}_w{k}", w_small[f"l{i}_w{k}"], A[f"l{i}_w{k}"])
        load("l2_fc", w_mlp["l2"][0], A["l2_fc"])
        load("l2_pr", w_mlp["l2"][1], A["l2_pr"])

        pool.do(step(nc.gpsimd.memset, minus_half[:, :], -0.5))
        t_ones = pool.do(step(nc.gpsimd.memset, ones[:, :], 1.0))
        t_ones_row = pool.do(step(nc.gpsimd.memset, ones_row[:, :], 1.0))
        for hd, ring in vdiag.items():
            for i, v in enumerate(ring.bufs):
                t = pool.do(step(nc.gpsimd.memset, v, 0.0), pool.now())
                t = pool.do(step(nc.gpsimd.memset, v[0:S, :, 2 * hd:2 * hd + 1], 1.0), t)
                t = pool.do(step(nc.gpsimd.memset, v[S:P, :, 2 * hd + 1:2 * hd + 2], 1.0), t)
                ring.free[i] = [t]
        t_pool_consts = pool.now()
        t_gate = act.do(step(nc.scalar.activation, tanh_gate[:, :], col("gate"), ACT.Tanh), loads["cols"])
        LOWEST = -3.3895313892515355e38
        t_min = dve.do(step(nc.vector.tensor_scalar, mask_row["l2"][:, :], mask_u8[:, :], -1.0, -LOWEST, ALU.add,
                                                 ALU.mult), loads["mask"])
        t_inf = dve.do(step(nc.vector.tensor_scalar, mask_row["l0"][:, :], mask_row["l2"][:, :], -LOWEST, None,
                                                 ALU.mult), t_min)

        x_ready = [[loads["x0"] if b < 2 else loads["x1"]] for b in range(B)]

        def normalise(src, dst, eps, st, after, tiles):
            for t in range(tiles):
                s = st[:, 16 * t:16 * t + 16]
                t0 = dve.do(step(nc.vector.bn_stats, s[:, 0:6], src[:, t, :]), *after)
                t1 = dve.do(step(nc.vector.bn_aggr, s[:, 6:8], s[:, 0:6]), t0)
            per_tile = st[:, 0:16 * tiles].rearrange("p (t k) -> p t k", k=16)
            var, var_eps, rstd = per_tile[:, :, 7], per_tile[:, :, 8], per_tile[:, :, 9]
            t2 = dve.do(step(nc.vector.tensor_scalar, var_eps, var, eps, None, ALU.add), t1)
            t3 = pool.do(step(nc.gpsimd.tensor_tensor, rstd, var_eps, minus_half[:, 0:tiles], ALU.pow), t2,
                         t_pool_consts)
            for t in range(tiles):
                s = st[:, 16 * t:16 * t + 16]
                last = dve.do(step(nc.vector.tensor_scalar, dst[:, t, :], src[:, t, :], s[:, 6:7], s[:, 9:10],
                                   ALU.subtract, ALU.mult), t3)
            return last

        def transpose_tiles(src, after):
            bank, free, i = work.take()
            parts = [step(nc.tensor.transpose, bank[:, c * T + t * P:c * T + (t + 1) * P],
                                                     src[:, t, c * P:(c + 1) * P], ident[:, :])
                     for t in range(TT) for c in range(DC)]
            tok = pe.run(parts, *free, *after, loads["ident"])
            return bank, tok, i

        def affine_evac(bank, tok, i, dst, free, gamma=None, beta=None):
            if gamma is None and beta is None:
                t = act.do(step(nc.scalar.activation, dst, bank[:, :].rearrange("p (c t) -> p c t", c=DC), ACT.Copy),
                           tok, *free)
            else:
                for c in range(DC):
                    src = bank[:, c * T:(c + 1) * T]
                    if gamma is None:
                        t = act.do(step(nc.scalar.activation, dst[:, c, :], src, ACT.Identity,
                                                                        bias=col(beta, c)),
                                   tok, *free, loads["cols"])
                    else:
                        t = dve.do(step(nc.vector.tensor_scalar, 
                            dst[:, c, :], src, col(gamma, c), col(beta, c), ALU.mult, ALU.add),
                            tok, *free, loads["cols"])
            work.release(i, t)
            return t

        st, _, i_st = stat.take()
        t_norm = normalise(ctx_raw, ctx_norm, 1e-5, st, [loads["ctx"]], CTX // P)
        stat.release(i_st, t_norm)
        t_ctxT, t_aT = [], []
        for src, dst, after, toks in ((ctx_raw, ctxT, [loads["ctx"]], t_ctxT), (ctx_norm, aT, [t_norm], t_aT)):
            for c in range(DC):
                bank, free, i = work.take()
                tok = pe.run([step(nc.tensor.transpose, 
                    bank[:, n * P:(n + 1) * P], src[:, n, c * P:(c + 1) * P], ident[:, :])
                    for n in range(CTX // P)], *free, *after, loads["ident"])
                if src is ctx_raw:
                    t = act.do(step(nc.scalar.activation, ctxT[:, c, :], bank[:, :], ACT.Copy), tok)
                else:
                    t = dve.do(step(nc.vector.tensor_scalar, aT[:, c, :], bank[:, :], col("l0_g", c),
                                                                         col("l0_b", c), ALU.mult, ALU.add),
                               tok, loads["cols"])
                toks.append(t)
                work.release(i, t)

        LAYERS = {
            "l0": dict(i=0, hd=16, scale=0.25, src=aT, src_ready=t_aT, bq=None, bk=None, bv=None),
            "l1": dict(i=1, hd=8, scale=8.0 ** -0.5, src=ctxT, src_ready=t_ctxT, bq="l1_bq", bk="l1_bk",
                       bv="l1_bv"),
            "l2": dict(i=2, hd=16, scale=0.25, src=ctxT, src_ready=t_ctxT, bq="l2_bq", bk="l2_bk", bv="l2_bv"),
        }

        def small_keys(name):
            L = LAYERS[name]
            kT, toks = kT_small[L["i"]], []
            for o in range(DC):
                bank, free, i = work.take()
                w = w_small[f"{name}_wk"]
                tok = pe.run([step(nc.tensor.matmul, 
                    bank[:, :], w[:, c, o * P:(o + 1) * P], L["src"][:, c, :], start=(c == 0), stop=(c == DC - 1))
                    for c in range(DC)], *free, *L["src_ready"], loads[f"{name}_wk"])
                if L["bk"]:
                    t = act.do(step(nc.scalar.activation, kT[:, o, :], bank[:, :], ACT.Identity,
                                                                      bias=col(L["bk"], o)), tok, loads["cols"])
                else:
                    t = act.do(step(nc.scalar.activation, kT[:, o, :], bank[:, :], ACT.Copy), tok)
                toks.append(t)
                work.release(i, t)
            L["kT_ready"] = toks
            yield

        def small_attention(name, b):
            L = LAYERS[name]
            hd, w = L["hd"], {k: w_small[f"{name}_w{k}"] for k in "qvo"}
            heads = D // hd
            chunk_heads = P // hd
            pairs, vw = heads // 2, 2 * hd + 2
            xb = x[:, TT * b:TT * (b + 1), :]

            kd, kd_free, i_kd = kdiag.take()
            kT = kT_small[L["i"]]
            for c in range(DC):
                t_kd = pool.do(step(nc.gpsimd.tensor_tensor, 
                    kd[:, c, 0:chunk_heads * S].rearrange("p (h s) -> p h s", s=S),
                    kT[:, c, b * S:(b + 1) * S].unsqueeze(1).broadcast_to([P, chunk_heads, S]),
                    head_of_row[hd].unsqueeze(2).broadcast_to([P, chunk_heads, S]), ALU.mult),
                    *kd_free, *L["kT_ready"], loads["maskhead"], loads["maskhead8"])

            bank, free, i = work.take()
            tok = pe.run([step(nc.tensor.matmul, 
                bank[j * S:(j + 1) * S, 0:D], L["src"][:, c, b * S:(b + 1) * S], w["v"][:, c, :],
                start=(c == 0), stop=(c == DC - 1), skip_group_check=True)
                for c in range(DC) for j in range(2)], *free, *L["src_ready"], loads[f"{name}_wv"])
            vd, vd_free, i_vd = vdiag[hd].take()
            t_vd = []
            for j in range(2):
                src = bank[j * S:(j + 1) * S, 0:D].rearrange("p (q j d) -> p q j d", j=2, d=hd)[:, :, j, :]
                dst = vd[j * S:(j + 1) * S, :, j * hd:(j + 1) * hd]
                if L["bv"]:
                    bias = row(L["bv"])[j * S:(j + 1) * S, :].rearrange("p (q j d) -> p q j d", j=2, d=hd)[:, :, j, :]
                    t_vd.append(dve.do(step(nc.vector.tensor_tensor, dst, src, bias, ALU.add),
                                       tok, *vd_free, loads["rows_early"]))
                else:
                    t_vd.append(dve.do(step(nc.vector.tensor_copy, dst, src), tok, *vd_free))
            work.release(i, *t_vd)
            yield

            after = x_ready[b]
            if name == "l2":
                st, st_free, i_st = stat.take()
                xn, xn_free, i_xn = norm_ring.take()
                t_x = normalise(xb, xn, 1e-5, st, [*after, *st_free, *xn_free], TT)
                stat.release(i_st, t_x)
                bank, tok, i = transpose_tiles(xn, [t_x])
                norm_ring.release(i_xn, tok)
            else:
                bank, tok, i = transpose_tiles(xb, after)
                t_x = tok
            sT, sT_free, i_sT = srcT_ring.take()
            t_sT = affine_evac(bank, tok, i, sT, sT_free, *(("l2_g1", "l2_b1") if name == "l2" else ()))
            if name != "l0":
                t_xb = pool.do(step(nc.gpsimd.tensor_tensor, 
                    xb, xb, row(f"{name}_bo").unsqueeze(1).broadcast_to([P, TT, D]), ALU.add),
                    *after, t_x, loads["rows_early"], loads["rows_late"])
            else:
                t_xb = None
            yield

            bank, free, i = work.take()
            tok = pe.run([step(nc.tensor.matmul, 
                bank[:, o * T:(o + 1) * T], w["q"][:, c, o * P:(o + 1) * P], sT[:, c, :], start=(c == 0),
                stop=(c == DC - 1)) for o in range(DC) for c in range(DC)], *free, t_sT, loads[f"{name}_wq"])
            srcT_ring.release(i_sT, tok)
            qT, qT_free, i_qT = qT_ring.take()
            t_qT = affine_evac(bank, tok, i, qT, qT_free, None, L["bq"])
            yield

            o_buf, o_free, i_o = o_ring.take()
            t_o = []
            for t in range(TT):
                for g in range(heads // GH):
                    sc, sc_free, i_sc = score_ring.take()
                    parts = []
                    for half in range(2):
                        c, k0 = (half, 0) if chunk_heads == 8 else (g, half * BANK)
                        parts.append(step(nc.tensor.matmul, 
                            sc[:, half * BANK:(half + 1) * BANK], qT[:, c, t * P:(t + 1) * P],
                            kd[:, c, k0:k0 + BANK], start=True, stop=(name == "l1")))
                        if name != "l1":
                            parts.append(step(nc.tensor.matmul, 
                                sc[:, half * BANK:(half + 1) * BANK], ones_row[:, :],
                                mask_row[name][:, b * S:(b + 1) * S].unsqueeze(1).broadcast_to([1, 8, S]),
                                start=False, stop=True))
                    tok = pe.run(parts, *sc_free, t_qT, t_kd, t_ones_row, t_inf)
                    st, st_free, i_st = stat.take()
                    pr, pr_free, i_pr = probs.take()
                    e3 = pr[:, 0:GS].rearrange("p (h s) -> p h s", s=S)
                    s3 = sc[:, :].rearrange("p (h s) -> p h s", s=S)
                    bmax = st[:, 0:GH].unsqueeze(2).broadcast_to([P, GH, S])
                    if name == "l1":
                        msk = mask_tok[:, TT * b + t, :].unsqueeze(1).broadcast_to([P, GH, S])
                        t0 = dve.do(step(nc.vector.scalar_tensor_tensor, out=e3, in0=s3, scalar=L["scale"], in1=msk,
                                                                     op0=ALU.mult, op1=ALU.add),
                                    tok, *pr_free, loads["mask_tok"])
                        score_ring.release(i_sc, t0)
                        t1 = dve.do(step(nc.vector.tensor_reduce, st[:, 0:GH], e3, X, ALU.max), t0, *st_free)
                        t2 = dve.do(step(nc.vector.tensor_tensor, e3, e3, bmax, ALU.subtract), t1)
                    else:
                        t1 = dve.do(step(nc.vector.tensor_reduce, st[:, 0:GH], s3, X, ALU.max), tok, *st_free)
                        t2 = dve.do(step(nc.vector.tensor_tensor, e3, s3, bmax, ALU.subtract), t1, *pr_free)
                        score_ring.release(i_sc, t2)
                    stat.release(i_st, t2)
                    scale = 1.0 if name == "l1" else L["scale"]
                    t_e = act.do(step(nc.scalar.activation, pr[:, 0:GS], pr[:, 0:GS], ACT.Exp, scale=scale), t2)
                    yield

                    pT, pT_free, i_pT = probsT.take()
                    t_pT = []
                    for half in range(2):
                        bank, free, i = work.take()
                        tok = pe.run([step(nc.tensor.transpose, 
                            bank[:, q * P:(q + 1) * P], pr[:, (4 * half + q) * P:(4 * half + q + 1) * P],
                            ident[:, :]) for q in range(4)], *free, t_e)
                        dst = pT[:, 4 * half:4 * half + 4, :].rearrange("p q t -> p (q t)")
                        if half == 0:
                            t2 = act.do(step(nc.scalar.activation, dst, bank[:, :], ACT.Copy),
                                        tok, *pT_free)
                        else:
                            t2 = dve.do(step(nc.vector.tensor_copy, dst, bank[:, :]), tok, *pT_free)
                        t_pT.append(t2)
                        work.release(i, t2)
                    probs.release(i_pr, tok)
                    yield

                    bank, free, i = work.take()
                    tok = pe.run([step(nc.tensor.matmul, 
                        bank[:, q * vw:(q + 1) * vw], pT[:, q, :], vd[:, 8 * g + q, :], start=True, stop=True)
                        for q in range(8)], *free, *t_pT, *t_vd)
                    probsT.release(i_pT, tok)
                    st, st_free, i_st = stat.take()
                    b3 = bank[:, 0:8 * vw].rearrange("p (q w) -> p q w", w=vw)
                    t0 = dve.do(step(nc.vector.reciprocal, st[:, 0:GH].rearrange("p (q j) -> p q j", j=2),
                                                       b3[:, :, 2 * hd:vw]), tok, *st_free)
                    t1 = dve.do(step(nc.vector.tensor_tensor, 
                        o_buf[:, t, g * GH * hd:(g + 1) * GH * hd].rearrange("p (q j d) -> p q j d", j=2, d=hd),
                        b3[:, :, 0:2 * hd].rearrange("p q (j d) -> p q j d", j=2),
                        st[:, 0:GH].rearrange("p (q j) -> p q j", j=2).unsqueeze(3).broadcast_to([P, 8, 2, hd]),
                        ALU.mult), t0, *o_free)
                    work.release(i, t1)
                    stat.release(i_st, t1)
                    t_o.append(t1)
                    yield
            qT_ring.release(i_qT, pe.now())
            kdiag.release(i_kd, pe.now())
            vdiag[hd].release(i_vd, pe.now())

            bank, tok, i = transpose_tiles(o_buf, t_o)
            o_ring.release(i_o, tok)
            oT, oT_free, i_oT = oT_ring.take()
            t_oT = affine_evac(bank, tok, i, oT, oT_free)
            yield
            bank, free, i = work.take()
            tok = pe.run([step(nc.tensor.matmul, 
                bank[:, t * D:(t + 1) * D], oT[:, c, t * P:(t + 1) * P], w["o"][:, c, :], start=(c == 0),
                stop=(c == DC - 1)) for t in range(TT) for c in range(DC)], *free, t_oT, loads[f"{name}_wo"])
            oT_ring.release(i_oT, tok)
            y3 = bank[:, :].rearrange("p (t d) -> p t d", t=TT)
            if name == "l0":
                t_x = dve.do(step(nc.vector.scalar_tensor_tensor, out=xb, in0=y3, scalar=tanh_gate[:, 0:1], in1=xb,
                                                              op0=ALU.mult, op1=ALU.add), tok, t_gate)
                work.release(i, t_x)
            else:
                t_x = dve.do(step(nc.vector.tensor_tensor, xb, y3, xb, ALU.add), tok, t_xb)
                work.release(i, t_x)
            if name == "l1":
                st, st_free, i_st = stat.take()
                t1 = normalise(xb, xb, 1e-6, st, [t_x, *st_free], TT)
                stat.release(i_st, t1)
                t2 = pool.do(step(nc.gpsimd.tensor_tensor, 
                    xb, xb, row("l1_g").unsqueeze(1).broadcast_to([P, TT, D]), ALU.mult), t1)
                t_x = pool.do(step(nc.gpsimd.tensor_tensor, 
                    xb, xb, row("l1_b").unsqueeze(1).broadcast_to([P, TT, D]), ALU.add), t2)
            x_ready[b] = [t_x]
            yield

        def mlp(b, w1, w2, ready, gamma, beta, fcb, pb, func, hidden, store):
            xb = x[:, TT * b:TT * (b + 1), :]
            st, st_free, i_st = stat.take()
            xn, xn_free, i_xn = norm_ring.take()
            t_n = normalise(xb, xn, 1e-5, st, [*x_ready[b], *st_free, *xn_free], TT)
            stat.release(i_st, t_n)
            t_xb = pool.do(step(nc.gpsimd.tensor_tensor, xb, xb, row(pb).unsqueeze(1).broadcast_to([P, TT, D]),
                                                     ALU.add), t_n, loads["rows_late"])
            bank, tok, i = transpose_tiles(xn, [t_n])
            norm_ring.release(i_xn, tok)
            sT, sT_free, i_sT = srcT_ring.take()
            t_sT = affine_evac(bank, tok, i, sT, sT_free, gamma, beta)
            yield
            hid, hid_free, i_hid = hidden.take()
            t_h = []
            for f in range(0, FC, 2):
                bank, free, i = work.take()
                tok = pe.run([step(nc.tensor.matmul, 
                    bank[:, j * T:(j + 1) * T], w1[:, c, (f + j) * P:(f + j + 1) * P], sT[:, c, :],
                    start=(c == 0), stop=(c == DC - 1)) for j in range(2) for c in range(DC)],
                    *free, t_sT, *ready)
                for j in range(2):
                    t = act.do(step(nc.scalar.activation, 
                        hid[:, f + j, :], bank[:, j * T:(j + 1) * T], func, bias=col(fcb, f + j)), tok, *hid_free)
                t_h.append(t)
                work.release(i, t)
                if f == 2:
                    yield
            srcT_ring.release(i_sT, tok)
            yield
            bank, free, i = work.take()
            tok = pe.run([step(nc.tensor.matmul, 
                bank[:, t * D:(t + 1) * D], hid[:, f, t * P:(t + 1) * P], w2[:, f, :], start=(f == 0),
                stop=(f == FC - 1)) for t in range(TT) for f in range(FC)], *free, *t_h)
            hidden.release(i_hid, tok)
            t_x = dve.do(step(nc.vector.tensor_tensor, xb, bank[:, :].rearrange("p (t d) -> p t d", t=TT), xb,
                                                   ALU.add), tok, t_xb)
            work.release(i, t_x)
            x_ready[b] = [t_x]
            if store:
                dst = out.rearrange("(n p) d -> p n d", p=P)[:, TT * b:TT * (b + 1), :]
                sp.wait([t_x])
                sp.todo.append(lambda e: e.dma_start(dst, xb).then_inc(s_out, 16))
            yield

        WN = H3 * D
        w3_wq = w3[:, 0:WN].rearrange("p (h d) -> p h d", h=H3)
        w3_wk = w3[:, WN:2 * WN].rearrange("p (c n) -> p c n", c=DC)
        w3_wv = w3[:, 2 * WN:3 * WN].rearrange("p (c n) -> p c n", c=DC)
        w3_wo = w3[:, 3 * WN:4 * WN].rearrange("p (h d) -> p h d", h=H3)
        SCALE3 = float(K3) ** -0.5
        n_kq, n_vo = DC * GS, GH // 2 * D
        pk = [p[:, 0:2 * n_kq].rearrange("p (b c n) -> p b c n", b=2, c=DC) for p in pair]
        pv = [p[:, 2 * n_kq:2 * (n_kq + n_vo)].rearrange("p (b q d) -> p b q d", b=2, q=GH // 2) for p in pair]
        pc = [p[:, 2 * (n_kq + n_vo):].rearrange("p (b n) -> p b n", b=2) for p in pair]
        w3_free, pair_free, bias_free = [], [[], []], []
        pair_ready = {}
        bias_ready = {}

        def load_w3(a):
            for k, n in (("k", 1), ("q", 0), ("v", 2), ("o", 3)):
                load(f"l3_w{k}{a}", w3[:, n * WN:(n + 1) * WN], A[f"l3_w{k}{a}"], *w3_free)

        def l3_bias(a):
            bank, free, i = work.take()
            tok = pe.run([step(nc.tensor.matmul, 
                bank[:, c * H3 + h:c * H3 + h + 1], w3_wq[:, h, c * P:(c + 1) * P], col(f"l3_kb{a}", h),
                start=True, stop=True) for c in range(DC) for h in range(H3)], *free, loads[f"l3_wq{a}"],
                loads["cols"])
            t_k = dve.do(step(nc.vector.tensor_copy, kbias[:, :, :].rearrange("p c h -> p (c h)"), bank[:, 0:DC * H3]),
                         tok, *bias_free)
            work.release(i, t_k)
            prod, prod_free, i_pr = stat.take()
            t0 = dve.do(step(nc.vector.tensor_tensor, prod[:, 0:H3], col(f"l3_bq{a}", 0, H3), col(f"l3_kb{a}", 0, H3),
                                                  ALU.mult), *prod_free)
            bank2, free, i = work.take()
            tok = pe.run([step(nc.tensor.matmul, bank2[:, 0:H3], ones[:, :], prod[:, 0:H3], start=True, stop=True)],
                         *free, t0, t_ones)
            t_c = dve.do(step(nc.vector.tensor_copy, cbias[:, :], bank2[:, 0:H3]), tok)
            stat.release(i_pr, tok)
            work.release(i, t_c)
            yield
            diag, d_free, i_d = kvT.take()
            d2 = diag.rearrange("p a b -> p (a b)")[:, 0:H3 * H3]
            t0 = pool.do(step(nc.gpsimd.memset, d2, 0.0), *d_free)
            t1 = pool.do(step(nc.gpsimd.tensor_copy, d2[:, 0:H3 * H3:H3 + 1], col(f"l3_vb{a}", 0, H3)), t0,
                         loads["cols"])
            bank3, free, i = work.take()
            tok = pe.run([step(nc.tensor.matmul, bank3[0:H3, 0:D], d2[:, h * H3:(h + 1) * H3], w3_wo[:, h, :],
                                                  start=(h == 0), stop=(h == H3 - 1)) for h in range(H3)],
                         *free, t1, loads[f"l3_wo{a}"])
            t_v = dve.do(step(nc.vector.tensor_copy, vob[:, :], bank3[0:H3, 0:D]), tok)
            kvT.release(i_d, tok)
            work.release(i, t_v)
            bias_ready[a] = [t_k, t_c, t_v]
            yield

        def project_context(w, bias, hs, p, ready):
            bank, free, i = work.take()
            tok = pe.run([step(nc.tensor.matmul, 
                bank[:, h * P:(h + 1) * P], w[:, c, (hs + h) * K3:(hs + h + 1) * K3],
                ctxT[:, c, p * P:(p + 1) * P], start=(c == 0), stop=(c == DC - 1))
                for h in range(4) for c in range(DC)], *free, ready)
            dst, d_free, i_d = kvT.take()
            t = dve.do(step(nc.vector.tensor_tensor, 
                dst[:, :, :], bank[:, :].rearrange("p (h s) -> p h s", h=4),
                col(bias, hs, 4).unsqueeze(2).broadcast_to([P, 4, P]), ALU.add), tok, *d_free)
            work.release(i, t)
            return dst, t, i_d

        def l3_pair(a, p):
            s = p % 2
            free_pair = pair_free[s]
            ready = []
            for hs in range(0, H3, 4):
                kt, t_kt, i_kt = project_context(w3_wk, f"l3_bk{a}", hs, p, loads[f"l3_wk{a}"])
                yield
                for c in range(DC):
                    bank, free, i = work.take()
                    tok = pe.run([step(nc.tensor.matmul, 
                        bank[:, h * P:(h + 1) * P], w3_wq[:, hs + h, c * P:(c + 1) * P], kt[:, h, :], start=True,
                        stop=True) for h in range(4)], *free, t_kt, loads[f"l3_wq{a}"])
                    t = act.do(step(nc.scalar.activation, 
                        pk[s][:, :, c, hs * S:(hs + 4) * S].rearrange("p b (h k) -> p b h k", h=4),
                        bank[:, :].rearrange("p (h b k) -> p b h k", h=4, b=2), ACT.Copy), tok, *free_pair)
                    ready.append(t)
                    work.release(i, t)
                    yield
                bank, free, i = work.take()
                tok = pe.run([step(nc.tensor.matmul, 
                    bank[:, h * P:(h + 1) * P], col(f"l3_bq{a}", hs + h).broadcast_to([P, P]), kt[:, h, :],
                    start=True, stop=True) for h in range(4)], *free)
                t = act.do(step(nc.scalar.activation, 
                    pc[s][:, :, hs * S:(hs + 4) * S].rearrange("p b (h k) -> p b h k", h=4),
                    bank[:, :].rearrange("p (h b k) -> p b h k", h=4, b=2), ACT.Copy), tok, *free_pair)
                ready.append(t)
                work.release(i, t)
                kvT.release(i_kt, tok)
                yield
                vt, t_vt, i_vt = project_context(w3_wv, f"l3_bv{a}", hs, p, loads[f"l3_wv{a}"])
                yield
                for q in range(2):
                    bank, free, i = work.take()
                    tok = pe.run([step(nc.tensor.matmul, 
                        bank[j * S:(j + 1) * S, bb * D:(bb + 1) * D], vt[:, 2 * q + j, bb * S:(bb + 1) * S],
                        w3_wo[:, hs + 2 * q + j, :], start=True, stop=True, skip_group_check=True)
                        for bb in range(2) for j in range(2)], *free, t_vt, loads[f"l3_wo{a}"])
                    t = dve.do(step(nc.vector.tensor_copy, 
                        pv[s][:, :, hs // 2 + q, :], bank[:, :].rearrange("p (b d) -> p b d", b=2)),
                        tok, *free_pair)
                    ready.append(t)
                    work.release(i, t)
                kvT.release(i_vt, tok)
                yield
            pair_ready[a, p] = [act.now(), dve.now()]
            pair_free[s] = []

        def l3_attention(a, b):
            p, bb = divmod(b, 2)
            s = p % 2
            xb = x[:, TT * b:TT * (b + 1), :]
            st, st_free, i_st = stat.take()
            xn, xn_free, i_xn = norm_ring.take()
            t_n = normalise(xb, xn, 1e-5, st, [*x_ready[b], *st_free, *xn_free], TT)
            stat.release(i_st, t_n)
            t_xb = pool.do(step(nc.gpsimd.tensor_tensor, 
                xb, xb, row(f"l3_bo{a}").unsqueeze(1).broadcast_to([P, TT, D]), ALU.add), t_n)
            bank, tok, i = transpose_tiles(xn, [t_n])
            norm_ring.release(i_xn, tok)
            sT, sT_free, i_sT = srcT_ring.take()
            t_sT = affine_evac(bank, tok, i, sT, sT_free, f"l3_g{a}", f"l3_b{a}")
            yield
            for t in range(TT):
                sc, sc_free, i_sc = score_ring.take()
                bank, free, i = work.take()
                parts = [step(nc.tensor.matmul, 
                    sc[:, half * BANK:(half + 1) * BANK], sT[:, c, t * P:(t + 1) * P],
                    pk[s][:, bb, c, half * BANK:(half + 1) * BANK], start=(c == 0), stop=(c == DC - 1))
                    for half in range(2) for c in range(DC)]
                parts += [step(nc.tensor.matmul, bank[:, 0:H3], sT[:, c, t * P:(t + 1) * P], kbias[:, c, :],
                                                  start=(c == 0), stop=(c == DC - 1)) for c in range(DC)]
                tok = pe.run(parts, *sc_free, *free, t_sT, *pair_ready[a, p], *bias_ready[a])
                pr, pr_free, i_pr = probs.take()
                st, st_free, i_st = stat.take()
                e3 = pr[:, 0:GS].rearrange("p (h s) -> p h s", s=S)
                eb = pr[:, GS:GS + H3]
                m, den, r = st[:, 0:H3], st[:, 16:32], st[:, 32:48]

                def over_keys(v):
                    return v.unsqueeze(2).broadcast_to([P, H3, S])
                t_b = dve.do(step(nc.vector.tensor_tensor, eb, bank[:, 0:H3], cbias[:, :], ALU.add), tok, *pr_free)
                work.release(i, t_b)
                t0 = dve.do(step(nc.vector.tensor_tensor, pr[:, 0:GS], sc[:, :], pc[s][:, bb, :], ALU.add), tok)
                score_ring.release(i_sc, t0)
                t1 = dve.do(step(nc.vector.tensor_reduce, m, e3, X, ALU.max), t0, *st_free)
                t1 = dve.do(step(nc.vector.tensor_tensor, m, m, eb, ALU.max), t1, t_b)
                t2 = dve.do(step(nc.vector.tensor_tensor, e3, e3, over_keys(m), ALU.subtract), t1)
                t3 = dve.do(step(nc.vector.tensor_tensor, eb, eb, m, ALU.subtract), t1)
                t_e = act.do(step(nc.scalar.activation, pr[:, :], pr[:, :], ACT.Exp, scale=SCALE3), t2, t3)
                yield
                t4 = dve.do(step(nc.vector.tensor_reduce, den, e3, X, ALU.add), t_e)
                t5 = dve.do(step(nc.vector.tensor_tensor, den, den, eb, ALU.add), t4)
                t6 = dve.do(step(nc.vector.reciprocal, r, den), t5)
                t7 = pool.do(step(nc.gpsimd.tensor_tensor, e3, e3, over_keys(r), ALU.mult), t6)
                t8 = dve.do(step(nc.vector.tensor_tensor, eb, eb, r, ALU.mult), t6)
                stat.release(i_st, t7, t8)
                yield
                pT, pT_free, i_pT = probsT.take()
                t_pT = []
                for half in range(2):
                    bank, free, i = work.take()
                    tok = pe.run([step(nc.tensor.transpose, 
                        bank[:, q * P:(q + 1) * P], pr[:, (4 * half + q) * P:(4 * half + q + 1) * P],
                        ident[:, :]) for q in range(4)], *free, t7)
                    dst = pT[:, 4 * half:4 * half + 4, :].rearrange("p q t -> p (q t)")
                    t2 = act.do(step(nc.scalar.activation, dst, bank[:, :], ACT.Copy), tok, *pT_free)
                    t_pT.append(t2)
                    work.release(i, t2)
                bank, free, i = work.take()
                tok = pe.run([step(nc.tensor.transpose, bank[0:H3, 0:P], eb, ident[:, :])], *free, t8)
                t2 = dve.do(step(nc.vector.tensor_copy, pT[0:H3, GH // 2, :], bank[0:H3, 0:P]), tok, *pT_free)
                t_pT.append(t2)
                work.release(i, t2)
                probs.release(i_pr, tok)
                yield
                bank, free, i = work.take()
                parts = [step(nc.tensor.matmul, bank[:, 0:D], pT[:, q, :], pv[s][:, bb, q, :], start=(q == 0),
                                                 stop=False) for q in range(GH // 2)]
                parts.append(step(nc.tensor.matmul, bank[:, 0:D], pT[0:H3, GH // 2, :], vob[:, :], start=False,
                                                stop=True))
                tok = pe.run(parts, *free, *t_pT)
                probsT.release(i_pT, tok)
                t_x = dve.do(step(nc.vector.tensor_tensor, xb[:, t, :], bank[:, 0:D], xb[:, t, :], ALU.add),
                             tok, t_xb)
                work.release(i, t_x)
                yield
            srcT_ring.release(i_sT, pe.now())
            x_ready[b] = [t_x]
            pair_free[s] = [*pair_free[s], pe.now(), dve.now()]

        s_out = sem("s_out")

        small = [small_keys("l0")]
        for name in ("l0", "l1", "l2"):
            if name != "l0":
                small.insert(len(small) - 2, small_keys(name))
            small += [small_attention(name, b) for b in range(B)]
        interleave(small, 3)
        w3_free = so_far()
        load_w3(1)
        hid_l2 = Ring(hid_bufs, w3_free)
        probs, probsT = Ring(probs_bufs, w3_free), Ring(probsT_bufs, w3_free)
        mlps = [mlp(b, *w_mlp["l2"], [loads["l2_fc"], loads["l2_pr"]], "l2_g2", "l2_b2", "l2_fcb", "l2_pb",
                    ACT.Gelu_apprx_tanh, hid_l2, False) for b in range(B)]
        pair_free[0] = so_far()
        interleave(mlps[:5], 2)

        def first_pair():
            yield from l3_bias(1)
            yield from l3_pair(1, 0)
        beside(mlps[5:], first_pair(), 2, 2.0)
        pair_free[1] = so_far()
        srcT_ring = Ring([fixed[0], fixed[1]], so_far())
        norm_ring = Ring([fixed[2], fixed[3]], so_far())

        def after_first(*gens):
            for g in gens:
                yield from g
        for a in (1, 2):
            for p in range(B // 2):
                if p + 1 < B // 2:
                    side = l3_pair(a, p + 1)
                elif a == 1:
                    w3_free = so_far()
                    load_w3(2)
                    bias_free = []
                    side = l3_pair(2, 0)
                else:
                    side = iter(())
                if p == B // 2 - 1 and a == 2:
                    w3_free = so_far()
                    cut = carve(w3)
                    w_mlp["l3"] = (cut(DC, F), cut(FC, D))
                    hid_l3 = Ring([cut(FC, T) for _ in range(2)], w3_free)
                    load("l3_fc", w_mlp["l3"][0], A["l3_fc"], *w3_free)
                    load("l3_pr", w_mlp["l3"][1], A["l3_pr"], *w3_free)
                beside([l3_attention(a, 2 * p), l3_attention(a, 2 * p + 1)], side, 2, 1.6)
            if a == 1:
                bias_free = so_far()
                interleave([l3_bias(2)], 1)
        interleave([mlp(b, *w_mlp["l3"], [loads["l3_fc"], loads["l3_pr"]], "l3_gm", "l3_bm", "l3_fcb", "l3_pb",
                        ACT.Gelu, hid_l3, True) for b in range(B)], 2)

        with nc.Block() as block:
            @block.sync
            def _(e):
                sp.emit(e)
                e.wait_ge(s_out, 16 * B)

            @block.tensor
            def _(e):
                pe.emit(e)

            @block.vector
            def _(e):
                dve.emit(e)

            @block.scalar
            def _(e):
                act.emit(e)

            @block.gpsimd
            def _(e):
                pool.emit(e)


def kernel(**inputs):
    import numpy as np
    import concourse.bacc as bacc
    from concourse.bass_utils import run_bass_kernel_spmd

    v = {k: np.asarray(a) for k, a in inputs.items()}

    def rows_first(w):
        return np.ascontiguousarray(w.reshape(-1, P, w.shape[1]).transpose(1, 0, 2).reshape(P, -1))

    def per_group(w):
        w = w.reshape(-1, 8, 1, 8)
        return np.broadcast_to(w, (w.shape[0], 8, 4, 8)).reshape(w.shape[0], D)

    a = {"x": v["x"].reshape(B * T, D), "ctx": v["ctx_2048"].reshape(CTX, D),
         "mask": v["mask_BxS2_bf1"].view(np.uint8).reshape(1, CTX),
         "mask_tok": v["mask_Bx1xSxS2_ff0"].reshape(B * T, S)}
    for n, w in (("q", "Wq"), ("k", "Wk"), ("v", "Wv"), ("o", "Wo")):
        a[f"l0_w{n}"] = rows_first(v[f"L0_xattn_{w}"].T)
        m = v[f"L1_xattn_{w}"]
        a[f"l1_w{n}"] = rows_first(per_group(m) if n in "kv" else m)
        a[f"l2_w{n}"] = rows_first(v["L2_xattn_cproj_w" if n == "o" else f"L2_xattn_{n}_w"])
    a["l2_fc"], a["l2_pr"] = rows_first(v["L2_xattn_fc_w"]), rows_first(v["L2_xattn_proj_w"])
    a["l3_fc"], a["l3_pr"] = rows_first(v["L3_xattn_w_fc1"]), rows_first(v["L3_xattn_w_fc2"])
    for i in "12":
        a[f"l3_wq{i}"] = rows_first(v[f"L3_xattn_wq{i}"].T)
        for n in "kvo":
            a[f"l3_w{n}{i}"] = rows_first(v[f"L3_xattn_w{n}{i}"])
    named = {"l0_g": "L0_xattn_ln_gamma", "l0_b": "L0_xattn_ln_beta", "l1_bq": "L1_xattn_bq",
             "l2_g1": "L2_xattn_ln1_w", "l2_b1": "L2_xattn_ln1_b", "l2_bq": "L2_xattn_q_b", "l2_bk": "L2_xattn_k_b",
             "l2_g2": "L2_xattn_ln2_w", "l2_b2": "L2_xattn_ln2_b", "l2_fcb": "L2_xattn_fc_b",
             "l3_gm": "L3_xattn_ln_mlp_scale", "l3_bm": "L3_xattn_ln_mlp_offset", "l3_fcb": "L3_xattn_b_fc1"}
    for i in "12":
        named |= {f"l3_g{i}": f"L3_xattn_ln{i}_scale", f"l3_b{i}": f"L3_xattn_ln{i}_offset",
                  f"l3_bq{i}": f"L3_xattn_bq{i}", f"l3_bk{i}": f"L3_xattn_bk{i}", f"l3_bv{i}": f"L3_xattn_bv{i}",
                  f"l3_kb{i}": f"L3_xattn_bias_k{i}", f"l3_vb{i}": f"L3_xattn_bias_v{i}"}
    parts = []
    for n in COLS:
        if n == "gate":
            c = np.broadcast_to(v["L0_xattn_gate"].reshape(1, 1), (P, 1))
        elif n == "l1_bk":
            c = per_group(v["L1_xattn_bk"]).reshape(-1, P).T
        else:
            c = v[named[n]].reshape(-1, P).T
        parts.append(c)
    a["cols"] = np.ascontiguousarray(np.concatenate(parts, axis=1))
    rows = {"l1_bv": per_group(v["L1_xattn_bv"]), "l1_bo": v["L1_xattn_bo"], "l1_g": v["L1_xattn_gamma"],
            "l1_b": v["L1_xattn_beta"], "l2_bv": v["L2_xattn_v_b"], "l2_bo": v["L2_xattn_cproj_b"],
            "l2_pb": v["L2_xattn_proj_b"], "l3_bo1": v["L3_xattn_bo1"], "l3_bo2": v["L3_xattn_bo2"],
            "l3_pb": v["L3_xattn_b_fc2"]}
    a["rows"] = np.concatenate([rows[n].reshape(1, D) for n in ROWS], axis=0)
    a["ident"] = np.eye(P, dtype=np.float32)
    for hd in (16, 8):
        a[f"head{hd}"] = (np.arange(P)[:, None] // hd == np.arange(P // hd)[None, :]).astype(np.float32)

    nc = bacc.Bacc("TRN2", target_bir_lowering=False, num_devices=1)
    arrays, args = {}, {}
    for n, arr in a.items():
        arrays[f"in_{n}"] = np.ascontiguousarray(arr)
        args[n] = nc.dram_tensor(f"in_{n}", arr.shape, mybir.dt.from_np(arr.dtype), kind="ExternalInput").ap()
    out = nc.dram_tensor("out", (B * T, D), F32, kind="ExternalOutput").ap()
    build(nc, args, out)
    r = run_bass_kernel_spmd(nc, [arrays], core_ids=[0])
    return r.results[0]["out"].reshape(B, T, D)
```

```python
from contextlib import ExitStack
from functools import partial as step

import concourse.bass as bass
from concourse import mybir

F32 = mybir.dt.float32
BF16 = mybir.dt.bfloat16
U8 = mybir.dt.uint8
ALU = mybir.AluOpType
ACT = mybir.ActivationFunctionType
X = mybir.AxisListType.X

P = 128
D = 256
DC = D // P
B, T, S = 8, 256, 64
TT = T // P
CTX = B * S
H3, K3 = 16, 128
F = 4 * D
FC = F // P
GS = 1024
GH = GS // S
BANK = 512

COLS = {"l0_g": 2, "l0_b": 2, "gate": 1, "l1_bq": 2, "l1_bk": 2, "l2_g1": 2, "l2_b1": 2, "l2_bq": 2,
        "l2_bk": 2, "l2_g2": 2, "l2_b2": 2, "l2_fcb": FC, "l3_gm": 2, "l3_bm": 2, "l3_fcb": FC}
for _a in "12":
    COLS |= {f"l3_g{_a}": 2, f"l3_b{_a}": 2, f"l3_bq{_a}": H3, f"l3_bk{_a}": H3, f"l3_bv{_a}": H3,
             f"l3_kb{_a}": H3, f"l3_vb{_a}": H3}
COL_AT, _n = {}, 0
for _k, _v in COLS.items():
    COL_AT[_k] = _n
    _n += _v
N_COLS = _n
ROWS = ["l1_bv", "l1_bo", "l1_g", "l1_b", "l2_bv", "l2_bo", "l2_pb", "l3_bo1", "l3_bo2", "l3_pb"]
ROWS_EARLY = 6


class Engine:

    ends = {}
    LATENCY = 150

    def __init__(self, name, sem, cost):
        self.name, self.sem, self.count, self.todo, self.seen = name, sem, 0, [], {}
        self.cost, self.free_at = cost, 0

    def wait(self, tokens):
        self.free_at = max([self.free_at, *(ready_at(t) for t in tokens)])
        for sem, value in tokens:
            if self.seen.get(sem.name, 0) < value:
                self.seen[sem.name] = value
                self.todo.append(lambda e, s=sem, v=value: e.wait_ge(s, v))

    def do(self, what, *after):
        self.wait(after)
        self.count += 1
        self.free_at += self.cost(what)
        self.ends[self.sem.name, self.count] = self.free_at + self.LATENCY
        self.todo.append(lambda e: what().then_inc(self.sem, 1))
        return self.sem, self.count

    def run(self, parts, *after):
        self.wait(after)
        for what in parts[:-1]:
            self.free_at += self.cost(what)
            self.todo.append(lambda e, w=what: w())
        return self.do(parts[-1])

    def now(self):
        return self.sem, self.count

    def emit(self, e):
        for step in self.todo:
            step(e)


def elements(what):
    out = what.keywords.get("out", what.args[0] if what.args else None)
    n = 1
    for k in out.shape[1:]:
        n *= k
    return n


def ready_at(token):
    return Engine.ends.get((token[0].name, token[1]), 0)


class Ring:

    def __init__(self, bufs, free=()):
        self.bufs, self.free, self.order = list(bufs), [list(free) for _ in bufs], list(range(len(bufs)))

    def take(self):
        assert self.order, "every buffer is held"
        i = self.order.pop(0)
        return self.bufs[i], self.free[i], i

    def release(self, i, *tokens):
        self.free[i] = list(tokens)
        self.order.append(i)


def room(*needs):
    while any(len(ring.order) < n for ring, n in needs):
        yield BLOCKED


BLOCKED = "blocked"


def interleave(pe, streams, width, side=None):
    waiting, live = list(streams), []

    def advance(entry):
        tokens = next(entry[1], None)
        if tokens is None:
            entry[0] = None
        elif tokens is BLOCKED:
            entry[0] = BLOCKED
        else:
            entry[0] = max([0, *map(ready_at, tokens)])

    aside = [0, side] if side is not None else [None, None]
    while waiting or live or aside[0] is not None:
        while waiting and len(live) < width:
            live.append([0, waiting.pop(0)])
        for entry in [*live, aside]:
            if entry[0] is BLOCKED:
                advance(entry)
        live = [v for v in live if v[0] is not None]
        able = [v for v in live if v[0] is not BLOCKED]
        ready = [v for v in able if v[0] <= pe.free_at]
        if ready:
            pick = ready[0]
        elif aside[0] is not None and aside[0] is not BLOCKED:
            pick = aside
        elif able:
            pick = min(able, key=lambda v: v[0])
        else:
            assert waiting or not live, "every generator is blocked"
            continue
        advance(pick)
        live = [v for v in live if v[0] is not None]


def build(nc, A, out):
    ctx = ExitStack()
    with ctx:
        def sb(name, shape, dt=F32):
            return ctx.enter_context(nc.sbuf_tensor(name, shape, dt))

        def sem(name):
            return ctx.enter_context(nc.semaphore(name))

        score_ring = Ring([ctx.enter_context(nc.psum_tensor(f"scores{i}", [P, GS], F32)) for i in range(2)])
        work = Ring([ctx.enter_context(nc.psum_tensor(f"work{i}", [P, BANK], F32)) for i in range(4)])

        x = sb("x", [P, B * TT, D])
        ctxT = sb("ctxT", [P, DC, CTX])
        cols = sb("cols", [P, N_COLS])
        rows_late = sb("rows_late", [P, len(ROWS) - ROWS_EARLY, D])
        ident = sb("ident", [P, P])
        ones = sb("ones", [P, P])
        minus_half = sb("minus_half", [P, CTX // P])
        ones_row = sb("ones_row", [1, P], BF16)
        tanh_gate = sb("tanh_gate", [P, 1])
        probs_bufs = [sb(f"probs{i}", [P, GS + H3])[:, :] for i in range(2)]
        probsT_bufs = [sb(f"probsT{i}", [P, GH // 2 + 1, P])[:, :, :] for i in range(2)]
        stat = Ring([sb(f"stat{i}", [P, 48]) for i in range(12)])
        kvT = Ring([sb(f"kvT{i}", [P, 4, P]) for i in range(3)])
        w3 = sb("w3", [P, 4 * H3 * D])
        PAIR = 2 * (DC * GS + GH // 2 * D + GS)
        pair = [sb(f"pair{i}", [P, PAIR]) for i in range(2)]
        act_bufs = sb("act_bufs", [P, 4, DC * T])
        vob = sb("vob", [H3, D])
        kbias = sb("kbias", [P, DC, H3])
        cbias = sb("cbias", [P, H3])

        def carve(region):
            at = 0

            def cut(*shape):
                nonlocal at
                n = 1
                for s in shape:
                    n *= s
                assert at + n <= region.shape[1], "region full"
                v, at = region[:, at:at + n], at + n
                names = "abcd"[:len(shape)]
                if len(shape) == 1:
                    return v
                return v.rearrange(f"p ({' '.join(names)}) -> p {' '.join(names)}",
                                   **{k: s for k, s in zip(names, shape)})
            return cut

        cut = carve(w3)
        w_small = {f"l{i}_w{k}": cut(DC, D) for i in range(3) for k in "qkvo"}
        kT_small = [cut(DC, CTX) for _ in range(2)]
        kdiag = Ring([cut(DC, GS) for _ in range(4)])
        cut = carve(pair[0])
        ctx_region = cut(2 * CTX // P * D)
        aT = cut(DC, CTX)
        mask_tok = cut(B * TT, S)
        rows_early = cut(ROWS_EARLY, D)
        vdiag = {16: Ring([cut(8, 34) for _ in range(4)]), 8: Ring([cut(16, 18) for _ in range(3)])}
        qT_bufs = [cut(DC, T) for _ in range(3)]
        oT_ring = Ring([cut(DC, T) for _ in range(2)])
        head_of_row = {16: cut(8), 8: cut(16)}
        cut = carve(ctx_region)
        ctx_raw, ctx_norm = cut(CTX // P, D), cut(CTX // P, D)
        cut = carve(ctx_region)
        probs4, qT4, vdiag4 = cut(GS + H3), cut(DC, T), cut(16, 18)
        cut = carve(pair[1])
        w_mlp = {"l2": (cut(DC, F), cut(FC, D))}
        o4 = cut(DC, T)
        more = [cut(DC, T) for _ in range(2)]
        hid_and_probs = cut(2 * FC * T)
        cut = carve(hid_and_probs)
        probs3, probsT3 = cut(GS + H3), cut(GH // 2 + 1, P)
        o_bufs = [cut(DC, T) for _ in range(3)]
        cut = carve(hid_and_probs)
        hid_bufs = [cut(FC, T) for _ in range(2)]
        probs, probsT = Ring([*probs_bufs, probs3, probs4]), Ring([*probsT_bufs, probsT3])
        qT_ring = Ring([*qT_bufs, qT4])
        fixed = [act_bufs[:, i, :].rearrange("p (c t) -> p c t", c=DC) for i in range(4)]
        o_ring = Ring([*o_bufs, o4])
        srcT_ring = Ring([fixed[0], fixed[1], more[0]])
        norm_ring = Ring([fixed[2], fixed[3], more[1]])
        mask_u8 = sb("mask_u8", [1, CTX], U8)
        mask_row = {"l0": sb("mask_inf", [1, CTX], BF16), "l2": sb("mask_min", [1, CTX], BF16)}

        def pe_cost(what):
            n = max(elements(what), 60) / 2.4
            if what.func.__name__ == "transpose":
                return 2 * n
            return n if what.args[1].dtype == BF16 else 4 * n

        pe = Engine("pe", sem("s_pe"), pe_cost)
        dve = Engine("dve", sem("s_dve"), lambda what: 65 + elements(what) / 0.96)
        act = Engine("act", sem("s_act"), lambda what: 100 + elements(what) / 1.2)
        pool = Engine("pool", sem("s_pool"), lambda what: 60 + elements(what) * 2)
        sp = Engine("sp", None, None)
        engines = (pe, dve, act, pool)

        def so_far():
            return [e.now() for e in engines]

        loads = {}

        def load(name, dst, src, *after):
            loads[name] = (sem(f"in_{name}"), 16)
            sp.wait(after)
            sp.todo.append(lambda e, s=loads[name][0]: e.dma_start(dst, src).then_inc(s, 16))
            return loads[name]

        def col(name, i=0, n=1):
            return cols[:, COL_AT[name] + i:COL_AT[name] + i + n]

        def row(name):
            i = ROWS.index(name)
            return rows_early[:, i, :] if i < ROWS_EARLY else rows_late[:, i - ROWS_EARLY, :]

        load("ctx", ctx_raw, A["ctx"].rearrange("(n p) d -> p n d", p=P))
        load("ident", ident[:, :], A["ident"])
        load("cols", cols[:, :], A["cols"])
        load("maskhead", head_of_row[16], A["head16"])
        load("maskhead8", head_of_row[8], A["head8"])
        x_tiles = A["x"].rearrange("(n p) d -> p n d", p=P)
        for k in "kvqo":
            load(f"l0_w{k}", w_small[f"l0_w{k}"], A[f"l0_w{k}"])
            if k == "k":
                load("mask", mask_u8[:, :], A["mask"])
                load("x0", x[:, 0:4, :], x_tiles[:, 0:4, :])
        load("x1", x[:, 4:16, :], x_tiles[:, 4:16, :])
        load("rows_early", rows_early, A["rows"][0:ROWS_EARLY, :].unsqueeze(0).broadcast_to([P, ROWS_EARLY, D]))
        load("rows_late", rows_late[:, :, :],
             A["rows"][ROWS_EARLY:, :].unsqueeze(0).broadcast_to([P, len(ROWS) - ROWS_EARLY, D]))
        load("mask_tok", mask_tok, A["mask_tok"].rearrange("(n p) s -> p n s", p=P))
        for i in (1, 2):
            for k in "kvqo":
                load(f"l{i}_w{k}", w_small[f"l{i}_w{k}"], A[f"l{i}_w{k}"])
        load("l2_fc", w_mlp["l2"][0], A["l2_fc"])
        load("l2_pr", w_mlp["l2"][1], A["l2_pr"])

        pool.do(step(nc.gpsimd.memset, minus_half[:, :], -0.5))
        t_ones = pool.do(step(nc.gpsimd.memset, ones[:, :], 1.0))
        t_ones_row = pool.do(step(nc.gpsimd.memset, ones_row[:, :], 1.0))
        for hd, ring in vdiag.items():
            for i, v in enumerate(ring.bufs):
                t = pool.do(step(nc.gpsimd.memset, v, 0.0), pool.now())
                t = pool.do(step(nc.gpsimd.memset, v[0:S, :, 2 * hd:2 * hd + 1], 1.0), t)
                t = pool.do(step(nc.gpsimd.memset, v[S:P, :, 2 * hd + 1:2 * hd + 2], 1.0), t)
                ring.free[i] = [t]
        t_pool_consts = pool.now()
        t_gate = act.do(step(nc.scalar.activation, tanh_gate[:, :], col("gate"), ACT.Tanh), loads["cols"])
        LOWEST = -3.3895313892515355e38
        t_min = dve.do(step(nc.vector.tensor_scalar, mask_row["l2"][:, :], mask_u8[:, :], -1.0, -LOWEST, ALU.add,
                                                 ALU.mult), loads["mask"])
        t_inf = dve.do(step(nc.vector.tensor_scalar, mask_row["l0"][:, :], mask_row["l2"][:, :], -LOWEST, None,
                                                 ALU.mult), t_min)

        x_ready = [[loads["x0"] if b < 2 else loads["x1"]] for b in range(B)]

        def normalise(src, dst, eps, st, after, tiles):
            for t in range(tiles):
                s = st[:, 12 * t:12 * t + 12]
                t0 = dve.do(step(nc.vector.bn_stats, s[:, 0:6], src[:, t, :]), *after)
                t1 = dve.do(step(nc.vector.bn_aggr, s[:, 6:8], s[:, 0:6]), t0)
            per_tile = st[:, 0:12 * tiles].rearrange("p (t k) -> p t k", k=12)
            var, var_eps, rstd = per_tile[:, :, 7], per_tile[:, :, 8], per_tile[:, :, 9]
            t2 = dve.do(step(nc.vector.tensor_scalar, var_eps, var, eps, None, ALU.add), t1)
            t3 = pool.do(step(nc.gpsimd.tensor_tensor, rstd, var_eps, minus_half[:, 0:tiles], ALU.pow), t2,
                         t_pool_consts)
            yield [t3]
            for t in range(tiles):
                s = st[:, 12 * t:12 * t + 12]
                last = dve.do(step(nc.vector.tensor_scalar, dst[:, t, :], src[:, t, :], s[:, 6:7], s[:, 9:10],
                                   ALU.subtract, ALU.mult), t3)
            return last

        def transpose_tiles(src, after):
            bank, free, i = work.take()
            parts = [step(nc.tensor.transpose, bank[:, c * T + t * P:c * T + (t + 1) * P],
                                                     src[:, t, c * P:(c + 1) * P], ident[:, :])
                     for t in range(TT) for c in range(DC)]
            tok = pe.run(parts, *free, *after, loads["ident"])
            return bank, tok, i

        def affine_evac(bank, tok, i, dst, free, gamma=None, beta=None):
            if gamma is None and beta is None:
                t = act.do(step(nc.scalar.activation, dst, bank[:, :].rearrange("p (c t) -> p c t", c=DC), ACT.Copy),
                           tok, *free)
            else:
                for c in range(DC):
                    src = bank[:, c * T:(c + 1) * T]
                    if gamma is None:
                        t = act.do(step(nc.scalar.activation, dst[:, c, :], src, ACT.Identity,
                                                                        bias=col(beta, c)),
                                   tok, *free, loads["cols"])
                    else:
                        t = dve.do(step(nc.vector.tensor_scalar, 
                            dst[:, c, :], src, col(gamma, c), col(beta, c), ALU.mult, ALU.add),
                            tok, *free, loads["cols"])
            work.release(i, t)
            return t

        st, _, i_st = stat.take()
        def run_now(g):
            while True:
                try:
                    next(g)
                except StopIteration as end:
                    return end.value
        t_norm = run_now(normalise(ctx_raw, ctx_norm, 1e-5, st, [loads["ctx"]], CTX // P))
        stat.release(i_st, t_norm)
        t_ctxT, t_aT = [], []
        for src, dst, after, toks in ((ctx_raw, ctxT, [loads["ctx"]], t_ctxT), (ctx_norm, aT, [t_norm], t_aT)):
            for c in range(DC):
                bank, free, i = work.take()
                tok = pe.run([step(nc.tensor.transpose, 
                    bank[:, n * P:(n + 1) * P], src[:, n, c * P:(c + 1) * P], ident[:, :])
                    for n in range(CTX // P)], *free, *after, loads["ident"])
                if src is ctx_raw:
                    t = act.do(step(nc.scalar.activation, ctxT[:, c, :], bank[:, :], ACT.Copy), tok)
                else:
                    t = dve.do(step(nc.vector.tensor_scalar, aT[:, c, :], bank[:, :], col("l0_g", c),
                                                                         col("l0_b", c), ALU.mult, ALU.add),
                               tok, loads["cols"])
                toks.append(t)
                work.release(i, t)

        ctx_done = [*t_ctxT, *t_aT]
        probs.free[3], qT_ring.free[3] = ctx_done, ctx_done
        t = pool.do(step(nc.gpsimd.memset, vdiag4, 0.0), *ctx_done)
        t = pool.do(step(nc.gpsimd.memset, vdiag4[0:S, :, 16:17], 1.0), t)
        t = pool.do(step(nc.gpsimd.memset, vdiag4[S:P, :, 17:18], 1.0), t)
        vdiag[8].bufs.append(vdiag4)
        vdiag[8].free.append([t])
        vdiag[8].order.append(3)
        t_pool_consts = t

        LAYERS = {
            "l0": dict(i=0, hd=16, scale=0.25, src=aT, src_ready=t_aT, bq=None, bk=None, bv=None),
            "l1": dict(i=1, hd=8, scale=8.0 ** -0.5, src=ctxT, src_ready=t_ctxT, bq="l1_bq", bk="l1_bk",
                       bv="l1_bv"),
            "l2": dict(i=2, hd=16, scale=0.25, src=ctxT, src_ready=t_ctxT, bq="l2_bq", bk="l2_bk", bv="l2_bv"),
        }

        def small_keys(name):
            yield from room((work, 2))
            L = LAYERS[name]
            kT, toks = kT_small[L["i"] % 2], []
            kT_free = [pool.now()]
            for o in range(DC):
                bank, free, i = work.take()
                w = w_small[f"{name}_wk"]
                tok = pe.run([step(nc.tensor.matmul, 
                    bank[:, :], w[:, c, o * P:(o + 1) * P], L["src"][:, c, :], start=(c == 0), stop=(c == DC - 1))
                    for c in range(DC)], *free, *L["src_ready"], loads[f"{name}_wk"])
                if L["bk"]:
                    t = act.do(step(nc.scalar.activation, kT[:, o, :], bank[:, :], ACT.Identity,
                                                                      bias=col(L["bk"], o)), tok, *kT_free, loads["cols"])
                else:
                    t = act.do(step(nc.scalar.activation, kT[:, o, :], bank[:, :], ACT.Copy), tok, *kT_free)
                toks.append(t)
                work.release(i, t)
            L["kT_ready"] = toks
            yield []

        def small_attention(name, b):
            L = LAYERS[name]
            hd, w = L["hd"], {k: w_small[f"{name}_w{k}"] for k in "qvo"}
            heads = D // hd
            chunk_heads = P // hd
            pairs, vw = heads // 2, 2 * hd + 2
            xb = x[:, TT * b:TT * (b + 1), :]

            yield from room((kdiag, 1), (vdiag[hd], 1), (work, 1))
            kd, kd_free, i_kd = kdiag.take()
            kT = kT_small[L["i"] % 2]
            for c in range(DC):
                t_kd = pool.do(step(nc.gpsimd.tensor_tensor, 
                    kd[:, c, 0:chunk_heads * S].rearrange("p (h s) -> p h s", s=S),
                    kT[:, c, b * S:(b + 1) * S].unsqueeze(1).broadcast_to([P, chunk_heads, S]),
                    head_of_row[hd].unsqueeze(2).broadcast_to([P, chunk_heads, S]), ALU.mult),
                    *kd_free, *L["kT_ready"], loads["maskhead"], loads["maskhead8"])

            bank, free, i = work.take()
            tok = pe.run([step(nc.tensor.matmul, 
                bank[j * S:(j + 1) * S, 0:D], L["src"][:, c, b * S:(b + 1) * S], w["v"][:, c, :],
                start=(c == 0), stop=(c == DC - 1), skip_group_check=True)
                for c in range(DC) for j in range(2)], *free, *L["src_ready"], loads[f"{name}_wv"])
            vd, vd_free, i_vd = vdiag[hd].take()
            t_vd = []
            for j in range(2):
                src = bank[j * S:(j + 1) * S, 0:D].rearrange("p (q j d) -> p q j d", j=2, d=hd)[:, :, j, :]
                dst = vd[j * S:(j + 1) * S, :, j * hd:(j + 1) * hd]
                if L["bv"]:
                    bias = row(L["bv"])[j * S:(j + 1) * S, :].rearrange("p (q j d) -> p q j d", j=2, d=hd)[:, :, j, :]
                    t_vd.append(dve.do(step(nc.vector.tensor_tensor, dst, src, bias, ALU.add),
                                       tok, *vd_free, loads["rows_early"]))
                else:
                    t_vd.append(dve.do(step(nc.vector.tensor_copy, dst, src), tok, *vd_free))
            work.release(i, *t_vd)
            yield x_ready[b]
            yield from room((norm_ring, 1), (stat, 1))

            after = x_ready[b]
            if name == "l2":
                st, st_free, i_st = stat.take()
                xn, xn_free, i_xn = norm_ring.take()
                t_x = yield from normalise(xb, xn, 1e-5, st, [*after, *st_free, *xn_free], TT)
                stat.release(i_st, t_x)
                yield [t_x]
                yield from room((work, 1), (srcT_ring, 1))
                bank, tok, i = transpose_tiles(xn, [t_x])
                norm_ring.release(i_xn, tok)
            else:
                yield from room((work, 1), (srcT_ring, 1))
                bank, tok, i = transpose_tiles(xb, after)
                t_x = tok
            sT, sT_free, i_sT = srcT_ring.take()
            t_sT = affine_evac(bank, tok, i, sT, sT_free, *(("l2_g1", "l2_b1") if name == "l2" else ()))
            if name != "l0":
                t_xb = pool.do(step(nc.gpsimd.tensor_tensor, 
                    xb, xb, row(f"{name}_bo").unsqueeze(1).broadcast_to([P, TT, D]), ALU.add),
                    *after, t_x, loads["rows_early"], loads["rows_late"])
            else:
                t_xb = None
            yield [t_sT]

            yield from room((work, 1), (qT_ring, 1))
            bank, free, i = work.take()
            tok = pe.run([step(nc.tensor.matmul, 
                bank[:, o * T:(o + 1) * T], w["q"][:, c, o * P:(o + 1) * P], sT[:, c, :], start=(c == 0),
                stop=(c == DC - 1)) for o in range(DC) for c in range(DC)], *free, t_sT, loads[f"{name}_wq"])
            srcT_ring.release(i_sT, tok)
            qT, qT_free, i_qT = qT_ring.take()
            t_qT = affine_evac(bank, tok, i, qT, qT_free, None, L["bq"])
            yield [t_qT, t_kd]

            yield from room((o_ring, 1))
            o_buf, o_free, i_o = o_ring.take()
            t_o = []
            for t in range(TT):
                for g in range(heads // GH):
                    yield from room((score_ring, 1), (probs, 1), (stat, 1))
                    sc, sc_free, i_sc = score_ring.take()
                    parts = []
                    for half in range(2):
                        c, k0 = (half, 0) if chunk_heads == 8 else (g, half * BANK)
                        parts.append(step(nc.tensor.matmul, 
                            sc[:, half * BANK:(half + 1) * BANK], qT[:, c, t * P:(t + 1) * P],
                            kd[:, c, k0:k0 + BANK], start=True, stop=(name == "l1")))
                        if name != "l1":
                            parts.append(step(nc.tensor.matmul, 
                                sc[:, half * BANK:(half + 1) * BANK], ones_row[:, :],
                                mask_row[name][:, b * S:(b + 1) * S].unsqueeze(1).broadcast_to([1, 8, S]),
                                start=False, stop=True))
                    tok = pe.run(parts, *sc_free, t_qT, t_kd, t_ones_row, t_inf)
                    yield [tok]
                    st, st_free, i_st = stat.take()
                    pr, pr_free, i_pr = probs.take()
                    e3 = pr[:, 0:GS].rearrange("p (h s) -> p h s", s=S)
                    s3 = sc[:, :].rearrange("p (h s) -> p h s", s=S)
                    bmax = st[:, 0:GH].unsqueeze(2).broadcast_to([P, GH, S])
                    if name == "l1":
                        msk = mask_tok[:, TT * b + t, :].unsqueeze(1).broadcast_to([P, GH, S])
                        t0 = dve.do(step(nc.vector.scalar_tensor_tensor, out=e3, in0=s3, scalar=L["scale"], in1=msk,
                                                                     op0=ALU.mult, op1=ALU.add),
                                    tok, *pr_free, loads["mask_tok"])
                        score_ring.release(i_sc, t0)
                        t1 = dve.do(step(nc.vector.tensor_reduce, st[:, 0:GH], e3, X, ALU.max), t0, *st_free)
                        t2 = dve.do(step(nc.vector.tensor_tensor, e3, e3, bmax, ALU.subtract), t1)
                    else:
                        t1 = dve.do(step(nc.vector.tensor_reduce, st[:, 0:GH], s3, X, ALU.max), tok, *st_free)
                        t2 = dve.do(step(nc.vector.tensor_tensor, e3, s3, bmax, ALU.subtract), t1, *pr_free)
                        score_ring.release(i_sc, t2)
                    stat.release(i_st, t2)
                    yield [t2]
                    scale = 1.0 if name == "l1" else L["scale"]
                    t_e = act.do(step(nc.scalar.activation, pr[:, 0:GS], pr[:, 0:GS], ACT.Exp, scale=scale), t2)
                    yield [t_e]

                    yield from room((probsT, 1), (work, 2))
                    pT, pT_free, i_pT = probsT.take()
                    t_pT = []
                    for half in range(2):
                        bank, free, i = work.take()
                        tok = pe.run([step(nc.tensor.transpose, 
                            bank[:, q * P:(q + 1) * P], pr[:, (4 * half + q) * P:(4 * half + q + 1) * P],
                            ident[:, :]) for q in range(4)], *free, t_e)
                        dst = pT[:, 4 * half:4 * half + 4, :].rearrange("p q t -> p (q t)")
                        t2 = act.do(step(nc.scalar.activation, dst, bank[:, :], ACT.Copy), tok, *pT_free)
                        t_pT.append(t2)
                        work.release(i, t2)
                    probs.release(i_pr, tok)
                    yield t_pT

                    yield from room((work, 1), (stat, 1))
                    bank, free, i = work.take()
                    tok = pe.run([step(nc.tensor.matmul, 
                        bank[:, q * vw:(q + 1) * vw], pT[:, q, :], vd[:, 8 * g + q, :], start=True, stop=True)
                        for q in range(8)], *free, *t_pT, *t_vd)
                    probsT.release(i_pT, tok)
                    yield [tok]
                    st, st_free, i_st = stat.take()
                    b3 = bank[:, 0:8 * vw].rearrange("p (q w) -> p q w", w=vw)
                    t0 = dve.do(step(nc.vector.reciprocal, st[:, 0:GH].rearrange("p (q j) -> p q j", j=2),
                                                       b3[:, :, 2 * hd:vw]), tok, *st_free)
                    t1 = dve.do(step(nc.vector.tensor_tensor, 
                        o_buf[:, t, g * GH * hd:(g + 1) * GH * hd].rearrange("p (q j d) -> p q j d", j=2, d=hd),
                        b3[:, :, 0:2 * hd].rearrange("p q (j d) -> p q j d", j=2),
                        st[:, 0:GH].rearrange("p (q j) -> p q j", j=2).unsqueeze(3).broadcast_to([P, 8, 2, hd]),
                        ALU.mult), t0, *o_free)
                    work.release(i, t1)
                    stat.release(i_st, t1)
                    t_o.append(t1)
                    yield [t1] if t == TT - 1 and g == heads // GH - 1 else []
            qT_ring.release(i_qT, pe.now())
            kdiag.release(i_kd, pe.now())
            vdiag[hd].release(i_vd, pe.now())

            yield from room((work, 1), (oT_ring, 1))
            bank, tok, i = transpose_tiles(o_buf, t_o)
            o_ring.release(i_o, tok)
            oT, oT_free, i_oT = oT_ring.take()
            t_oT = affine_evac(bank, tok, i, oT, oT_free)
            yield [t_oT]
            yield from room((work, 1))
            bank, free, i = work.take()
            tok = pe.run([step(nc.tensor.matmul, 
                bank[:, t * D:(t + 1) * D], oT[:, c, t * P:(t + 1) * P], w["o"][:, c, :], start=(c == 0),
                stop=(c == DC - 1)) for t in range(TT) for c in range(DC)], *free, t_oT, loads[f"{name}_wo"])
            oT_ring.release(i_oT, tok)
            yield [tok]
            y3 = bank[:, :].rearrange("p (t d) -> p t d", t=TT)
            if name == "l0":
                t_x = dve.do(step(nc.vector.scalar_tensor_tensor, out=xb, in0=y3, scalar=tanh_gate[:, 0:1], in1=xb,
                                                              op0=ALU.mult, op1=ALU.add), tok, t_gate)
                work.release(i, t_x)
            else:
                t_x = dve.do(step(nc.vector.tensor_tensor, xb, y3, xb, ALU.add), tok, t_xb)
                work.release(i, t_x)
            if name == "l1":
                yield from room((stat, 1))
                st, st_free, i_st = stat.take()
                t1 = yield from normalise(xb, xb, 1e-6, st, [t_x, *st_free], TT)
                stat.release(i_st, t1)
                yield [t1]
                t2 = pool.do(step(nc.gpsimd.tensor_tensor, 
                    xb, xb, row("l1_g").unsqueeze(1).broadcast_to([P, TT, D]), ALU.mult), t1)
                t_x = pool.do(step(nc.gpsimd.tensor_tensor, 
                    xb, xb, row("l1_b").unsqueeze(1).broadcast_to([P, TT, D]), ALU.add), t2)
            x_ready[b] = [t_x]
            yield []

        def mlp(b, w1, w2, ready, gamma, beta, fcb, pb, func, hidden, store):
            xb = x[:, TT * b:TT * (b + 1), :]
            yield from room((stat, 1), (norm_ring, 1))
            st, st_free, i_st = stat.take()
            xn, xn_free, i_xn = norm_ring.take()
            t_n = yield from normalise(xb, xn, 1e-5, st, [*x_ready[b], *st_free, *xn_free], TT)
            stat.release(i_st, t_n)
            t_xb = pool.do(step(nc.gpsimd.tensor_tensor, xb, xb, row(pb).unsqueeze(1).broadcast_to([P, TT, D]),
                                                     ALU.add), t_n, loads["rows_late"])
            yield [t_n]
            yield from room((work, 1), (srcT_ring, 1))
            bank, tok, i = transpose_tiles(xn, [t_n])
            norm_ring.release(i_xn, tok)
            sT, sT_free, i_sT = srcT_ring.take()
            t_sT = affine_evac(bank, tok, i, sT, sT_free, gamma, beta)
            yield [t_sT]
            yield from room((hidden, 1))
            hid, hid_free, i_hid = hidden.take()
            t_h = []
            for f in range(0, FC, 2):
                yield from room((work, 1))
                bank, free, i = work.take()
                tok = pe.run([step(nc.tensor.matmul, 
                    bank[:, j * T:(j + 1) * T], w1[:, c, (f + j) * P:(f + j + 1) * P], sT[:, c, :],
                    start=(c == 0), stop=(c == DC - 1)) for j in range(2) for c in range(DC)],
                    *free, t_sT, *ready)
                for j in range(2):
                    t = act.do(step(nc.scalar.activation, 
                        hid[:, f + j, :], bank[:, j * T:(j + 1) * T], func, bias=col(fcb, f + j)), tok, *hid_free)
                t_h.append(t)
                work.release(i, t)
                yield []
            srcT_ring.release(i_sT, tok)
            yield t_h
            yield from room((work, 1))
            bank, free, i = work.take()
            tok = pe.run([step(nc.tensor.matmul, 
                bank[:, t * D:(t + 1) * D], hid[:, f, t * P:(t + 1) * P], w2[:, f, :], start=(f == 0),
                stop=(f == FC - 1)) for t in range(TT) for f in range(FC)], *free, *t_h)
            hidden.release(i_hid, tok)
            yield [tok]
            t_x = dve.do(step(nc.vector.tensor_tensor, xb, bank[:, :].rearrange("p (t d) -> p t d", t=TT), xb,
                                                   ALU.add), tok, t_xb)
            work.release(i, t_x)
            x_ready[b] = [t_x]
            if store:
                dst = out.rearrange("(n p) d -> p n d", p=P)[:, TT * b:TT * (b + 1), :]
                sp.wait([t_x])
                sp.todo.append(lambda e: e.dma_start(dst, xb).then_inc(s_out, 16))
            yield []

        WN = H3 * D
        w3_wq = w3[:, 0:WN].rearrange("p (h d) -> p h d", h=H3)
        w3_wk = w3[:, WN:2 * WN].rearrange("p (c n) -> p c n", c=DC)
        w3_wv = w3[:, 2 * WN:3 * WN].rearrange("p (c n) -> p c n", c=DC)
        w3_wo = w3[:, 3 * WN:4 * WN].rearrange("p (h d) -> p h d", h=H3)
        SCALE3 = float(K3) ** -0.5
        n_kq, n_vo = DC * GS, GH // 2 * D
        pk = [p[:, 0:2 * n_kq].rearrange("p (b c n) -> p b c n", b=2, c=DC) for p in pair]
        pv = [p[:, 2 * n_kq:2 * (n_kq + n_vo)].rearrange("p (b q d) -> p b q d", b=2, q=GH // 2) for p in pair]
        pc = [p[:, 2 * (n_kq + n_vo):].rearrange("p (b n) -> p b n", b=2) for p in pair]
        w3_free, pair_users = [], {}
        pair_ready = {}
        bias_ready = {}

        def load_w3(a):
            for k, n in (("k", 1), ("q", 0), ("v", 2), ("o", 3)):
                load(f"l3_w{k}{a}", w3[:, n * WN:(n + 1) * WN], A[f"l3_w{k}{a}"], *w3_free)

        def l3_bias(a):
            bank, free, i = work.take()
            tok = pe.run([step(nc.tensor.matmul, 
                bank[:, c * H3 + h:c * H3 + h + 1], w3_wq[:, h, c * P:(c + 1) * P], col(f"l3_kb{a}", h),
                start=True, stop=True) for c in range(DC) for h in range(H3)], *free, loads[f"l3_wq{a}"],
                loads["cols"])
            t_k = dve.do(step(nc.vector.tensor_copy, kbias[:, :, :].rearrange("p c h -> p (c h)"), bank[:, 0:DC * H3]),
                         tok)
            work.release(i, t_k)
            prod, prod_free, i_pr = stat.take()
            t0 = dve.do(step(nc.vector.tensor_tensor, prod[:, 0:H3], col(f"l3_bq{a}", 0, H3), col(f"l3_kb{a}", 0, H3),
                                                  ALU.mult), *prod_free)
            bank2, free, i = work.take()
            tok = pe.run([step(nc.tensor.matmul, bank2[:, 0:H3], ones[:, :], prod[:, 0:H3], start=True, stop=True)],
                         *free, t0, t_ones)
            t_c = dve.do(step(nc.vector.tensor_copy, cbias[:, :], bank2[:, 0:H3]), tok)
            stat.release(i_pr, tok)
            work.release(i, t_c)
            yield []
            diag, d_free, i_d = kvT.take()
            d2 = diag.rearrange("p a b -> p (a b)")[:, 0:H3 * H3]
            t0 = pool.do(step(nc.gpsimd.memset, d2, 0.0), *d_free)
            t1 = pool.do(step(nc.gpsimd.tensor_copy, d2[:, 0:H3 * H3:H3 + 1], col(f"l3_vb{a}", 0, H3)), t0,
                         loads["cols"])
            bank3, free, i = work.take()
            tok = pe.run([step(nc.tensor.matmul, bank3[0:H3, 0:D], d2[:, h * H3:(h + 1) * H3], w3_wo[:, h, :],
                                                  start=(h == 0), stop=(h == H3 - 1)) for h in range(H3)],
                         *free, t1, loads[f"l3_wo{a}"])
            t_v = dve.do(step(nc.vector.tensor_copy, vob[:, :], bank3[0:H3, 0:D]), tok)
            kvT.release(i_d, tok)
            work.release(i, t_v)
            bias_ready[a] = [t_k, t_c, t_v]
            yield []

        def project_context(w, bias, hs, p, ready):
            yield from room((work, 1), (kvT, 1))
            bank, free, i = work.take()
            tok = pe.run([step(nc.tensor.matmul, 
                bank[:, h * P:(h + 1) * P], w[:, c, (hs + h) * K3:(hs + h + 1) * K3],
                ctxT[:, c, p * P:(p + 1) * P], start=(c == 0), stop=(c == DC - 1))
                for h in range(4) for c in range(DC)], *free, ready)
            dst, d_free, i_d = kvT.take()
            t = dve.do(step(nc.vector.tensor_tensor, 
                dst[:, :, :], bank[:, :].rearrange("p (h s) -> p h s", h=4),
                col(bias, hs, 4).unsqueeze(2).broadcast_to([P, 4, P]), ALU.add), tok, *d_free)
            work.release(i, t)
            return dst, t, i_d

        def l3_pair(a, p):
            s = p % 2
            while len(pair_users[s]) < 2:
                yield BLOCKED
            free_pair = [t for user in pair_users[s] for t in user]
            pair_users[s] = []
            ready = []
            for hs in range(0, H3, 4):
                kt, t_kt, i_kt = yield from project_context(w3_wk, f"l3_bk{a}", hs, p, loads[f"l3_wk{a}"])
                yield [t_kt]
                for c in range(DC):
                    yield from room((work, 1))
                    bank, free, i = work.take()
                    tok = pe.run([step(nc.tensor.matmul, 
                        bank[:, h * P:(h + 1) * P], w3_wq[:, hs + h, c * P:(c + 1) * P], kt[:, h, :], start=True,
                        stop=True) for h in range(4)], *free, t_kt, loads[f"l3_wq{a}"])
                    t = act.do(step(nc.scalar.activation, 
                        pk[s][:, :, c, hs * S:(hs + 4) * S].rearrange("p b (h k) -> p b h k", h=4),
                        bank[:, :].rearrange("p (h b k) -> p b h k", h=4, b=2), ACT.Copy), tok, *free_pair)
                    ready.append(t)
                    work.release(i, t)
                    yield []
                yield from room((work, 1))
                bank, free, i = work.take()
                tok = pe.run([step(nc.tensor.matmul, 
                    bank[:, h * P:(h + 1) * P], col(f"l3_bq{a}", hs + h).broadcast_to([P, P]), kt[:, h, :],
                    start=True, stop=True) for h in range(4)], *free)
                t = act.do(step(nc.scalar.activation, 
                    pc[s][:, :, hs * S:(hs + 4) * S].rearrange("p b (h k) -> p b h k", h=4),
                    bank[:, :].rearrange("p (h b k) -> p b h k", h=4, b=2), ACT.Copy), tok, *free_pair)
                ready.append(t)
                work.release(i, t)
                kvT.release(i_kt, tok)
                yield []
                vt, t_vt, i_vt = yield from project_context(w3_wv, f"l3_bv{a}", hs, p, loads[f"l3_wv{a}"])
                yield [t_vt]
                for q in range(2):
                    yield from room((work, 1))
                    bank, free, i = work.take()
                    tok = pe.run([step(nc.tensor.matmul, 
                        bank[j * S:(j + 1) * S, bb * D:(bb + 1) * D], vt[:, 2 * q + j, bb * S:(bb + 1) * S],
                        w3_wo[:, hs + 2 * q + j, :], start=True, stop=True, skip_group_check=True)
                        for bb in range(2) for j in range(2)], *free, t_vt, loads[f"l3_wo{a}"])
                    t = dve.do(step(nc.vector.tensor_copy, 
                        pv[s][:, :, hs // 2 + q, :], bank[:, :].rearrange("p (b d) -> p b d", b=2)),
                        tok, *free_pair)
                    ready.append(t)
                    work.release(i, t)
                kvT.release(i_vt, tok)
                yield []
            pair_ready[a, p] = [act.now(), dve.now()]

        def l3_attention(a, b):
            p, bb = divmod(b, 2)
            s = p % 2
            while (a, p) not in pair_ready:
                yield BLOCKED
            xb = x[:, TT * b:TT * (b + 1), :]
            yield from room((stat, 1), (norm_ring, 1))
            st, st_free, i_st = stat.take()
            xn, xn_free, i_xn = norm_ring.take()
            t_n = yield from normalise(xb, xn, 1e-5, st, [*x_ready[b], *st_free, *xn_free], TT)
            stat.release(i_st, t_n)
            t_xb = pool.do(step(nc.gpsimd.tensor_tensor, 
                xb, xb, row(f"l3_bo{a}").unsqueeze(1).broadcast_to([P, TT, D]), ALU.add), t_n)
            yield [t_n]
            yield from room((work, 1), (srcT_ring, 1))
            bank, tok, i = transpose_tiles(xn, [t_n])
            norm_ring.release(i_xn, tok)
            sT, sT_free, i_sT = srcT_ring.take()
            t_sT = affine_evac(bank, tok, i, sT, sT_free, f"l3_g{a}", f"l3_b{a}")
            yield [t_sT]
            for t in range(TT):
                yield from room((score_ring, 1), (work, 1), (probs, 1), (stat, 1))
                sc, sc_free, i_sc = score_ring.take()
                bank, free, i = work.take()
                parts = [step(nc.tensor.matmul, 
                    sc[:, half * BANK:(half + 1) * BANK], sT[:, c, t * P:(t + 1) * P],
                    pk[s][:, bb, c, half * BANK:(half + 1) * BANK], start=(c == 0), stop=(c == DC - 1))
                    for half in range(2) for c in range(DC)]
                parts += [step(nc.tensor.matmul, bank[:, 0:H3], sT[:, c, t * P:(t + 1) * P], kbias[:, c, :],
                                                  start=(c == 0), stop=(c == DC - 1)) for c in range(DC)]
                tok = pe.run(parts, *sc_free, *free, t_sT, *pair_ready[a, p], *bias_ready[a])
                yield [tok]
                pr, pr_free, i_pr = probs.take()
                st, st_free, i_st = stat.take()
                e3 = pr[:, 0:GS].rearrange("p (h s) -> p h s", s=S)
                eb = pr[:, GS:GS + H3]
                m, den, r = st[:, 0:H3], st[:, 16:32], st[:, 32:48]

                def over_keys(v):
                    return v.unsqueeze(2).broadcast_to([P, H3, S])
                t_b = dve.do(step(nc.vector.tensor_tensor, eb, bank[:, 0:H3], cbias[:, :], ALU.add), tok, *pr_free)
                work.release(i, t_b)
                t0 = dve.do(step(nc.vector.tensor_tensor, pr[:, 0:GS], sc[:, :], pc[s][:, bb, :], ALU.add), tok)
                score_ring.release(i_sc, t0)
                t1 = dve.do(step(nc.vector.tensor_reduce, m, e3, X, ALU.max), t0, *st_free)
                t1 = dve.do(step(nc.vector.tensor_tensor, m, m, eb, ALU.max), t1, t_b)
                t2 = dve.do(step(nc.vector.tensor_tensor, e3, e3, over_keys(m), ALU.subtract), t1)
                t3 = dve.do(step(nc.vector.tensor_tensor, eb, eb, m, ALU.subtract), t1)
                yield [t2]
                t_e = act.do(step(nc.scalar.activation, pr[:, :], pr[:, :], ACT.Exp, scale=SCALE3), t2, t3)
                yield [t_e]
                t4 = dve.do(step(nc.vector.tensor_reduce, den, e3, X, ALU.add), t_e)
                t5 = dve.do(step(nc.vector.tensor_tensor, den, den, eb, ALU.add), t4)
                t6 = dve.do(step(nc.vector.reciprocal, r, den), t5)
                t7 = pool.do(step(nc.gpsimd.tensor_tensor, e3, e3, over_keys(r), ALU.mult), t6)
                t8 = dve.do(step(nc.vector.tensor_tensor, eb, eb, r, ALU.mult), t6)
                stat.release(i_st, t7, t8)
                yield [t7]
                yield from room((probsT, 1), (work, 3))
                pT, pT_free, i_pT = probsT.take()
                t_pT = []
                for half in range(2):
                    bank, free, i = work.take()
                    tok = pe.run([step(nc.tensor.transpose, 
                        bank[:, q * P:(q + 1) * P], pr[:, (4 * half + q) * P:(4 * half + q + 1) * P],
                        ident[:, :]) for q in range(4)], *free, t7)
                    dst = pT[:, 4 * half:4 * half + 4, :].rearrange("p q t -> p (q t)")
                    t2 = act.do(step(nc.scalar.activation, dst, bank[:, :], ACT.Copy), tok, *pT_free)
                    t_pT.append(t2)
                    work.release(i, t2)
                bank, free, i = work.take()
                tok = pe.run([step(nc.tensor.transpose, bank[0:H3, 0:P], eb, ident[:, :])], *free, t8)
                t2 = dve.do(step(nc.vector.tensor_copy, pT[0:H3, GH // 2, :], bank[0:H3, 0:P]), tok, *pT_free)
                t_pT.append(t2)
                work.release(i, t2)
                probs.release(i_pr, tok)
                yield t_pT
                yield from room((work, 1))
                bank, free, i = work.take()
                parts = [step(nc.tensor.matmul, bank[:, 0:D], pT[:, q, :], pv[s][:, bb, q, :], start=(q == 0),
                                                 stop=False) for q in range(GH // 2)]
                parts.append(step(nc.tensor.matmul, bank[:, 0:D], pT[0:H3, GH // 2, :], vob[:, :], start=False,
                                                stop=True))
                tok = pe.run(parts, *free, *t_pT)
                probsT.release(i_pT, tok)
                yield [tok]
                t_x = dve.do(step(nc.vector.tensor_tensor, xb[:, t, :], bank[:, 0:D], xb[:, t, :], ALU.add),
                             tok, t_xb)
                work.release(i, t_x)
                yield []
            srcT_ring.release(i_sT, pe.now())
            x_ready[b] = [t_x]
            pair_users[s].append((pe.now(), dve.now()))

        s_out = sem("s_out")

        small = [small_keys("l0")]
        for name in ("l0", "l1", "l2"):
            if name != "l0":
                small.insert(len(small) - 2, small_keys(name))
            small += [small_attention(name, b) for b in range(B)]
        interleave(pe, small, 4)
        w3_free = so_far()
        load_w3(1)
        hid_l2 = Ring(hid_bufs, w3_free)
        probs, probsT = Ring(probs_bufs, w3_free), Ring(probsT_bufs, w3_free)
        pair_users[0] = [w3_free, []]
        mlps = [mlp(b, *w_mlp["l2"], [loads["l2_fc"], loads["l2_pr"]], "l2_g2", "l2_b2", "l2_fcb", "l2_pb",
                    ACT.Gelu_apprx_tanh, hid_l2, False) for b in range(B)]
        interleave(pe, mlps[:5], 2)

        def chain(*gens):
            for g in gens:
                yield from g
        interleave(pe, mlps[5:], 2, chain(l3_bias(1), l3_pair(1, 0)))
        pair_users[1] = [so_far(), []]
        srcT_ring = Ring([fixed[0], fixed[1]], so_far())
        norm_ring = Ring([fixed[2], fixed[3]], so_far())

        interleave(pe, [l3_attention(1, b) for b in range(6)], 2, chain(*(l3_pair(1, p) for p in (1, 2, 3))))
        w3_free = so_far()
        load_w3(2)
        interleave(pe, [l3_attention(1, b) for b in (6, 7)], 2, l3_pair(2, 0))
        interleave(pe, [], 1, l3_bias(2))
        interleave(pe, [l3_attention(2, b) for b in range(6)], 2, chain(*(l3_pair(2, p) for p in (1, 2, 3))))
        w3_free = so_far()
        cut = carve(w3)
        w_mlp["l3"] = (cut(DC, F), cut(FC, D))
        hid_l3 = Ring([cut(FC, T) for _ in range(2)], w3_free)
        load("l3_fc", w_mlp["l3"][0], A["l3_fc"], *w3_free)
        load("l3_pr", w_mlp["l3"][1], A["l3_pr"], *w3_free)
        interleave(pe, [l3_attention(2, b) for b in (6, 7)], 2)
        interleave(pe, [mlp(b, *w_mlp["l3"], [loads["l3_fc"], loads["l3_pr"]], "l3_gm", "l3_bm", "l3_fcb", "l3_pb",
                            ACT.Gelu, hid_l3, True) for b in range(B)], 2)

        with nc.Block() as block:
            @block.sync
            def _(e):
                sp.emit(e)
                e.wait_ge(s_out, 16 * B)

            @block.tensor
            def _(e):
                pe.emit(e)

            @block.vector
            def _(e):
                dve.emit(e)

            @block.scalar
            def _(e):
                act.emit(e)

            @block.gpsimd
            def _(e):
                pool.emit(e)


def kernel(**inputs):
    import numpy as np
    import concourse.bacc as bacc
    from concourse.bass_utils import run_bass_kernel_spmd

    v = {k: np.asarray(a) for k, a in inputs.items()}

    def rows_first(w):
        return np.ascontiguousarray(w.reshape(-1, P, w.shape[1]).transpose(1, 0, 2).reshape(P, -1))

    def per_group(w):
        w = w.reshape(-1, 8, 1, 8)
        return np.broadcast_to(w, (w.shape[0], 8, 4, 8)).reshape(w.shape[0], D)

    a = {"x": v["x"].reshape(B * T, D), "ctx": v["ctx_2048"].reshape(CTX, D),
         "mask": v["mask_BxS2_bf1"].view(np.uint8).reshape(1, CTX),
         "mask_tok": v["mask_Bx1xSxS2_ff0"].reshape(B * T, S)}
    for n, w in (("q", "Wq"), ("k", "Wk"), ("v", "Wv"), ("o", "Wo")):
        a[f"l0_w{n}"] = rows_first(v[f"L0_xattn_{w}"].T)
        m = v[f"L1_xattn_{w}"]
        a[f"l1_w{n}"] = rows_first(per_group(m) if n in "kv" else m)
        a[f"l2_w{n}"] = rows_first(v["L2_xattn_cproj_w" if n == "o" else f"L2_xattn_{n}_w"])
    a["l2_fc"], a["l2_pr"] = rows_first(v["L2_xattn_fc_w"]), rows_first(v["L2_xattn_proj_w"])
    a["l3_fc"], a["l3_pr"] = rows_first(v["L3_xattn_w_fc1"]), rows_first(v["L3_xattn_w_fc2"])
    for i in "12":
        a[f"l3_wq{i}"] = rows_first(v[f"L3_xattn_wq{i}"].T)
        for n in "kvo":
            a[f"l3_w{n}{i}"] = rows_first(v[f"L3_xattn_w{n}{i}"])
    named = {"l0_g": "L0_xattn_ln_gamma", "l0_b": "L0_xattn_ln_beta", "l1_bq": "L1_xattn_bq",
             "l2_g1": "L2_xattn_ln1_w", "l2_b1": "L2_xattn_ln1_b", "l2_bq": "L2_xattn_q_b", "l2_bk": "L2_xattn_k_b",
             "l2_g2": "L2_xattn_ln2_w", "l2_b2": "L2_xattn_ln2_b", "l2_fcb": "L2_xattn_fc_b",
             "l3_gm": "L3_xattn_ln_mlp_scale", "l3_bm": "L3_xattn_ln_mlp_offset", "l3_fcb": "L3_xattn_b_fc1"}
    for i in "12":
        named |= {f"l3_g{i}": f"L3_xattn_ln{i}_scale", f"l3_b{i}": f"L3_xattn_ln{i}_offset",
                  f"l3_bq{i}": f"L3_xattn_bq{i}", f"l3_bk{i}": f"L3_xattn_bk{i}", f"l3_bv{i}": f"L3_xattn_bv{i}",
                  f"l3_kb{i}": f"L3_xattn_bias_k{i}", f"l3_vb{i}": f"L3_xattn_bias_v{i}"}
    parts = []
    for n in COLS:
        if n == "gate":
            c = np.broadcast_to(v["L0_xattn_gate"].reshape(1, 1), (P, 1))
        elif n == "l1_bk":
            c = per_group(v["L1_xattn_bk"]).reshape(-1, P).T
        else:
            c = v[named[n]].reshape(-1, P).T
        parts.append(c)
    a["cols"] = np.ascontiguousarray(np.concatenate(parts, axis=1))
    rows = {"l1_bv": per_group(v["L1_xattn_bv"]), "l1_bo": v["L1_xattn_bo"], "l1_g": v["L1_xattn_gamma"],
            "l1_b": v["L1_xattn_beta"], "l2_bv": v["L2_xattn_v_b"], "l2_bo": v["L2_xattn_cproj_b"],
            "l2_pb": v["L2_xattn_proj_b"], "l3_bo1": v["L3_xattn_bo1"], "l3_bo2": v["L3_xattn_bo2"],
            "l3_pb": v["L3_xattn_b_fc2"]}
    a["rows"] = np.concatenate([rows[n].reshape(1, D) for n in ROWS], axis=0)
    a["ident"] = np.eye(P, dtype=np.float32)
    for hd in (16, 8):
        a[f"head{hd}"] = (np.arange(P)[:, None] // hd == np.arange(P // hd)[None, :]).astype(np.float32)

    nc = bacc.Bacc("TRN2", target_bir_lowering=False, num_devices=1)
    arrays, args = {}, {}
    for n, arr in a.items():
        arrays[f"in_{n}"] = np.ascontiguousarray(arr)
        args[n] = nc.dram_tensor(f"in_{n}", arr.shape, mybir.dt.from_np(arr.dtype), kind="ExternalInput").ap()
    out = nc.dram_tensor("out", (B * T, D), F32, kind="ExternalOutput").ap()
    build(nc, args, out)
    r = run_bass_kernel_spmd(nc, [arrays], core_ids=[0])
    return r.results[0]["out"].reshape(B, T, D)
```

```python
from contextlib import ExitStack
from functools import partial as step

import concourse.bass as bass
from concourse import mybir

F32 = mybir.dt.float32
F32R = mybir.dt.float32r
BF16 = mybir.dt.bfloat16
U8 = mybir.dt.uint8
ALU = mybir.AluOpType
ACT = mybir.ActivationFunctionType
X = mybir.AxisListType.X

P = 128
D = 256
DC = D // P
B, T, S = 8, 256, 64
TT = T // P
CTX = B * S
H3, K3 = 16, 128
F = 4 * D
FC = F // P
GS = 1024
GH = GS // S
BANK = 512

COLS = {"l0_g": 2, "l0_b": 2, "gate": 1, "l1_bq": 2, "l1_bk": 2, "l2_g1": 2, "l2_b1": 2, "l2_bq": 2,
        "l2_bk": 2, "l2_g2": 2, "l2_b2": 2, "l2_fcb": FC, "l3_gm": 2, "l3_bm": 2, "l3_fcb": FC}
for _a in "12":
    COLS |= {f"l3_g{_a}": 2, f"l3_b{_a}": 2, f"l3_bq{_a}": H3, f"l3_bk{_a}": H3, f"l3_bv{_a}": H3,
             f"l3_kb{_a}": H3, f"l3_vb{_a}": H3}
COL_AT, _n = {}, 0
for _k, _v in COLS.items():
    COL_AT[_k] = _n
    _n += _v
N_COLS = _n
ROWS = ["l1_bv", "l1_bo", "l1_g", "l1_b", "l2_bv", "l2_bo", "l2_pb", "l3_bo1", "l3_bo2", "l3_pb"]
ROWS_EARLY = 6


class Engine:

    ends = {}
    LATENCY = 250

    def __init__(self, name, sem, cost):
        self.name, self.sem, self.count, self.todo, self.seen = name, sem, 0, [], {}
        self.cost, self.free_at = cost, 0

    def wait(self, tokens):
        self.free_at = max([self.free_at, *(ready_at(t) for t in tokens)])
        for sem, value in tokens:
            if self.seen.get(sem.name, 0) < value:
                self.seen[sem.name] = value
                self.todo.append(lambda e, s=sem, v=value: e.wait_ge(s, v))

    def do(self, what, *after):
        self.wait(after)
        self.count += 1
        self.free_at += self.cost(what)
        self.ends[self.sem.name, self.count] = self.free_at + self.LATENCY
        self.todo.append(lambda e: what().then_inc(self.sem, 1))
        return self.sem, self.count

    def run(self, parts, *after):
        self.wait(after)
        for what in parts[:-1]:
            self.free_at += self.cost(what)
            self.todo.append(lambda e, w=what: w())
        return self.do(parts[-1])

    def now(self):
        return self.sem, self.count

    def emit(self, e):
        for step in self.todo:
            step(e)


def elements(what):
    out = what.keywords.get("out", what.args[0] if what.args else None)
    n = 1
    for k in out.shape[1:]:
        n *= k
    return n


def ready_at(token):
    return Engine.ends.get((token[0].name, token[1]), 0)


class Ring:

    def __init__(self, bufs, free=()):
        self.bufs, self.free, self.order = list(bufs), [list(free) for _ in bufs], list(range(len(bufs)))

    def take(self):
        assert self.order, "every buffer is held"
        i = self.order.pop(0)
        return self.bufs[i], self.free[i], i

    def release(self, i, *tokens):
        self.free[i] = list(tokens)
        self.order.append(i)


def room(*needs):
    while any(len(ring.order) < n for ring, n in needs):
        yield BLOCKED


class first(list):
    pass


BLOCKED = "blocked"


def interleave(pe, streams, width, *sides, young=False):
    waiting, live = list(streams), []
    aside = [[0, g, False] for g in sides]

    def advance(entry):
        tokens = next(entry[1], None)
        if tokens is None or tokens is BLOCKED:
            entry[0] = tokens
        else:
            entry[0] = max([0, *map(ready_at, tokens)])
            entry[2] = isinstance(tokens, first)

    while waiting or live or aside:
        while waiting and len(live) < width:
            live.append([0, waiting.pop(0), False])
        for entry in [*live, *aside]:
            if entry[0] is BLOCKED:
                advance(entry)
        live, aside = ([v for v in group if v[0] is not None] for group in (live, aside))
        able, able_aside = ([v for v in group if v[0] is not BLOCKED] for group in (live, aside))
        ready, ready_aside = ([v for v in group if v[0] <= pe.free_at] for group in (able, able_aside))
        if young:
            ready.reverse()
        order = [v for v in ready_aside + ready if v[2]] + ready + ready_aside
        if order:
            pick = order[0]
        elif able or able_aside:
            pick = min(able + able_aside, key=lambda v: v[0])
        else:
            assert waiting or not (live or aside), "every generator is blocked"
            continue
        advance(pick)
        live, aside = ([v for v in group if v[0] is not None] for group in (live, aside))


def build(nc, A, out):
    ctx = ExitStack()
    with ctx:
        def sb(name, shape, dt=F32):
            return ctx.enter_context(nc.sbuf_tensor(name, shape, dt))

        def sem(name):
            return ctx.enter_context(nc.semaphore(name))

        score_ring = Ring([ctx.enter_context(nc.psum_tensor(f"scores{i}", [P, GS], F32)) for i in range(2)])
        work = Ring([ctx.enter_context(nc.psum_tensor(f"work{i}", [P, BANK], F32)) for i in range(4)])

        w3 = sb("w3", [P, 4 * H3 * D])
        w3_at = nc.sbuf_base - 4 * w3.shape[1]
        PAIR = 2 * (DC * GS + GH // 2 * D + GS)
        pair, pair_at = [], []
        for i in range(2):
            pair.append(sb(f"pair{i}", [P, PAIR]))
            pair_at.append(nc.sbuf_base - 4 * PAIR)

        x = sb("x", [P, B * TT, D])
        ctxT = sb("ctxT", [P, DC, CTX])
        cols = sb("cols", [P, N_COLS])
        rows_late = sb("rows_late", [P, len(ROWS) - ROWS_EARLY, D])
        ident = sb("ident", [P, P])
        minus_half = sb("minus_half", [P, CTX // P])
        ones_row = sb("ones_row", [1, P], BF16)
        tanh_gate = sb("tanh_gate", [P, 1])
        probs_late = sb("probs_late", [P, GS + H3])
        probs_bufs = [sb(f"probs{i}", [P, GS + H3])[:, :] for i in range(2)]
        probsT_bufs = [sb(f"probsT{i}", [P, GH // 2, P])[:, :, :] for i in range(2)]
        stat = Ring([sb(f"stat{i}", [P, 48]) for i in range(12)])
        kvT = Ring([sb(f"kvT{i}", [P, 4, P]) for i in range(3)])
        act_bufs = sb("act_bufs", [P, 4, DC * T])

        def carve(region):
            at = 0

            def cut(*shape):
                nonlocal at
                n = 1
                for s in shape:
                    n *= s
                assert at + n <= region.shape[1], "region full"
                v, at = region[:, at:at + n], at + n
                names = "abcd"[:len(shape)]
                if len(shape) == 1:
                    return v
                return v.rearrange(f"p ({' '.join(names)}) -> p {' '.join(names)}",
                                   **{k: s for k, s in zip(names, shape)})
            return cut

        cut = carve(w3)
        w_small = {f"l{i}_w{k}": cut(DC, D) for i in range(3) for k in "qkvo"}
        kT_small = [cut(DC, CTX) for _ in range(2)]
        kdiag = Ring([cut(DC, GS) for _ in range(4)])
        cut = carve(pair[0])
        ctx_region = cut(2 * CTX // P * D)
        aT = cut(DC, CTX)
        mask_tok = cut(B * TT, S)
        rows_early = cut(ROWS_EARLY, D)
        vdiag = {16: Ring([cut(8, 34) for _ in range(4)]), 8: Ring([cut(16, 18) for _ in range(3)])}
        qT_bufs = [cut(DC, T) for _ in range(3)]
        oT_ring = Ring([cut(DC, T) for _ in range(2)])
        head_of_row = {16: cut(8), 8: cut(16)}
        cut = carve(ctx_region)
        ctx_raw, ctx_norm = cut(CTX // P, D), cut(CTX // P, D)
        cut = carve(ctx_region)
        probs4, qT4, vdiag4 = cut(GS + H3), cut(DC, T), cut(16, 18)
        cut = carve(pair[1])
        w_mlp = {"l2": (cut(DC, F), cut(FC, D))}
        o4 = cut(DC, T)
        more = [cut(DC, T) for _ in range(2)]
        hid_and_probs = cut(2 * FC * T)
        cut = carve(hid_and_probs)
        probs3, probsT3 = cut(GS + H3), cut(GH // 2, P)
        o_bufs = [cut(DC, T) for _ in range(3)]
        cut = carve(hid_and_probs)
        hid_bufs = [cut(FC, T) for _ in range(2)]
        probs, probsT = Ring([*probs_bufs, probs3, probs4]), Ring([*probsT_bufs, probsT3])
        qT_ring = Ring([*qT_bufs, qT4])
        fixed = [act_bufs[:, i, :].rearrange("p (c t) -> p c t", c=DC) for i in range(4)]
        o_ring = Ring([*o_bufs, o4])
        srcT_ring = Ring([fixed[0], fixed[1], more[0]])
        norm_ring = Ring([fixed[2], fixed[3], more[1]])
        mask_u8 = sb("mask_u8", [1, CTX], U8)
        at = pair_at[1] + 4 * PAIR - 2 * 2 * CTX
        mask_row = {name: nc.alloc_sbuf_tensor_at(f"mask_{name}", [1, CTX], BF16, offset=at + i * 2 * CTX)
                    for i, name in enumerate(("l0", "l2"))}

        def pe_cost(what):
            moving = max(elements(what), P) / 2.4
            if what.func.__name__ == "transpose":
                return 2 * moving
            if what.args[1].dtype in (BF16, F32R):
                return moving
            return (4 if what.args[0].shape[0] > P // 2 else 2.3) * moving

        pe = Engine("pe", sem("s_pe"), pe_cost)
        dve = Engine("dve", sem("s_dve"), lambda what: 65 + elements(what) / 0.96)
        act = Engine("act", sem("s_act"), lambda what: 100 + elements(what) / 1.2)
        pool = Engine("pool", sem("s_pool"), lambda what: 300 + elements(what) * 1.7)
        sp = Engine("sp", None, None)
        engines = (pe, dve, act, pool)

        def so_far():
            return [e.now() for e in engines]

        loads = {}
        BYTES_PER_NS = 220

        def load(name, dst, src, *after):
            loads[name] = (sem(f"in_{name}"), 16)
            sp.wait(after)
            n = 4
            for k in dst.shape:
                n *= k
            sp.free_at += n / BYTES_PER_NS
            Engine.ends[loads[name][0].name, 16] = sp.free_at + 2000
            sp.todo.append(lambda e, s=loads[name][0]: e.dma_start(dst, src).then_inc(s, 16))
            return loads[name]

        def col(name, i=0, n=1):
            return cols[:, COL_AT[name] + i:COL_AT[name] + i + n]

        def row(name):
            i = ROWS.index(name)
            return rows_early[:, i, :] if i < ROWS_EARLY else rows_late[:, i - ROWS_EARLY, :]

        load("ctx", ctx_raw, A["ctx"].rearrange("(n p) d -> p n d", p=P))
        load("ident", ident[:, :], A["ident"])
        load("cols", cols[:, :], A["cols"])
        load("maskhead", head_of_row[16], A["head16"])
        load("maskhead8", head_of_row[8], A["head8"])
        x_tiles = A["x"].rearrange("(n p) d -> p n d", p=P)
        for k in "kvqo":
            load(f"l0_w{k}", w_small[f"l0_w{k}"], A[f"l0_w{k}"])
            if k == "k":
                load("mask", mask_u8[:, :], A["mask"])
                load("x0", x[:, 0:4, :], x_tiles[:, 0:4, :])
        load("x1", x[:, 4:16, :], x_tiles[:, 4:16, :])
        load("rows_early", rows_early, A["rows"][0:ROWS_EARLY, :].unsqueeze(0).broadcast_to([P, ROWS_EARLY, D]))
        load("rows_late", rows_late[:, :, :],
             A["rows"][ROWS_EARLY:, :].unsqueeze(0).broadcast_to([P, len(ROWS) - ROWS_EARLY, D]))
        load("mask_tok", mask_tok, A["mask_tok"].rearrange("(n p) s -> p n s", p=P))
        for i in (1, 2):
            for k in "kvqo":
                load(f"l{i}_w{k}", w_small[f"l{i}_w{k}"], A[f"l{i}_w{k}"])
        load("l2_fc", w_mlp["l2"][0], A["l2_fc"])
        load("l2_pr", w_mlp["l2"][1], A["l2_pr"])

        pool.do(step(nc.gpsimd.memset, minus_half[:, :], -0.5))
        t_ones_row = pool.do(step(nc.gpsimd.memset, ones_row[:, :], 1.0))
        for hd, ring in vdiag.items():
            for i, v in enumerate(ring.bufs):
                t = pool.do(step(nc.gpsimd.memset, v, 0.0), pool.now())
                t = pool.do(step(nc.gpsimd.memset, v[0:S, :, 2 * hd:2 * hd + 1], 1.0), t)
                t = pool.do(step(nc.gpsimd.memset, v[S:P, :, 2 * hd + 1:2 * hd + 2], 1.0), t)
                ring.free[i] = [t]
        t_pool_consts = pool.now()
        t_gate = act.do(step(nc.scalar.activation, tanh_gate[:, :], col("gate"), ACT.Tanh), loads["cols"])
        LOWEST = -3.3895313892515355e38
        t_min = dve.do(step(nc.vector.tensor_scalar, mask_row["l2"][:, :], mask_u8[:, :], -1.0, -LOWEST, ALU.add,
                                                 ALU.mult), loads["mask"])
        t_inf = dve.do(step(nc.vector.tensor_scalar, mask_row["l0"][:, :], mask_row["l2"][:, :], -LOWEST, None,
                                                 ALU.mult), t_min)

        for a in "12":
            for k in "kv":
                t_differences = dve.do(step(nc.vector.tensor_tensor, col(f"l3_b{k}{a}", 0, H3),
                                            col(f"l3_b{k}{a}", 0, H3), col(f"l3_{k}b{a}", 0, H3), ALU.subtract),
                                       loads["cols"])

        x_ready = [[loads["x0"] if b < 2 else loads["x1"]] for b in range(B)]

        def normalise(src, dst, eps, st, after, tiles):
            for t in range(tiles):
                s = st[:, 12 * t:12 * t + 12]
                t0 = dve.do(step(nc.vector.bn_stats, s[:, 0:6], src[:, t, :]), *after)
                t1 = dve.do(step(nc.vector.bn_aggr, s[:, 6:8], s[:, 0:6]), t0)
            per_tile = st[:, 0:12 * tiles].rearrange("p (t k) -> p t k", k=12)
            var, var_eps, rstd = per_tile[:, :, 7], per_tile[:, :, 8], per_tile[:, :, 9]
            t2 = dve.do(step(nc.vector.tensor_scalar, var_eps, var, eps, None, ALU.add), t1)
            t3 = pool.do(step(nc.gpsimd.tensor_tensor, rstd, var_eps, minus_half[:, 0:tiles], ALU.pow), t2,
                         t_pool_consts)
            yield first([t3])
            for t in range(tiles):
                s = st[:, 12 * t:12 * t + 12]
                last = dve.do(step(nc.vector.tensor_scalar, dst[:, t, :], src[:, t, :], s[:, 6:7], s[:, 9:10],
                                   ALU.subtract, ALU.mult), t3)
            return last

        def transpose_tiles(src, after):
            bank, free, i = work.take()
            parts = [step(nc.tensor.transpose, bank[:, c * T + t * P:c * T + (t + 1) * P],
                                                     src[:, t, c * P:(c + 1) * P], ident[:, :])
                     for t in range(TT) for c in range(DC)]
            tok = pe.run(parts, *free, *after, loads["ident"])
            return bank, tok, i

        def affine_evac(bank, tok, i, dst, free, gamma=None, beta=None):
            if gamma is None and beta is None:
                t = act.do(step(nc.scalar.activation, dst, bank[:, :].rearrange("p (c t) -> p c t", c=DC), ACT.Copy),
                           tok, *free)
            else:
                for c in range(DC):
                    src = bank[:, c * T:(c + 1) * T]
                    if gamma is None:
                        t = act.do(step(nc.scalar.activation, dst[:, c, :], src, ACT.Identity,
                                                                        bias=col(beta, c)),
                                   tok, *free, loads["cols"])
                    else:
                        t = dve.do(step(nc.vector.tensor_scalar,
                            dst[:, c, :], src, col(gamma, c), col(beta, c), ALU.mult, ALU.add),
                            tok, *free, loads["cols"])
            work.release(i, t)
            return t

        st, _, i_st = stat.take()
        def run_now(g):
            while True:
                try:
                    next(g)
                except StopIteration as end:
                    return end.value
        t_norm = run_now(normalise(ctx_raw, ctx_norm, 1e-5, st, [loads["ctx"]], CTX // P))
        stat.release(i_st, t_norm)
        t_ctxT, t_aT = [], []
        for src, dst, after, toks in ((ctx_raw, ctxT, [loads["ctx"]], t_ctxT), (ctx_norm, aT, [t_norm], t_aT)):
            for c in range(DC):
                bank, free, i = work.take()
                tok = pe.run([step(nc.tensor.transpose,
                    bank[:, n * P:(n + 1) * P], src[:, n, c * P:(c + 1) * P], ident[:, :])
                    for n in range(CTX // P)], *free, *after, loads["ident"])
                if src is ctx_raw:
                    t = act.do(step(nc.scalar.activation, ctxT[:, c, :], bank[:, :], ACT.Copy), tok)
                else:
                    t = dve.do(step(nc.vector.tensor_scalar, aT[:, c, :], bank[:, :], col("l0_g", c),
                                                                         col("l0_b", c), ALU.mult, ALU.add),
                               tok, loads["cols"])
                toks.append(t)
                work.release(i, t)

        ctx_done = [*t_ctxT, *t_aT]
        probs.free[3], qT_ring.free[3] = ctx_done, ctx_done
        t = pool.do(step(nc.gpsimd.memset, vdiag4, 0.0), *ctx_done)
        t = pool.do(step(nc.gpsimd.memset, vdiag4[0:S, :, 16:17], 1.0), t)
        t = pool.do(step(nc.gpsimd.memset, vdiag4[S:P, :, 17:18], 1.0), t)
        vdiag[8].bufs.append(vdiag4)
        vdiag[8].free.append([t])
        vdiag[8].order.append(3)
        t_pool_consts = t

        LAYERS = {
            "l0": dict(i=0, hd=16, scale=0.25, src=aT, src_ready=t_aT, bq=None, bk=None, bv=None),
            "l1": dict(i=1, hd=8, scale=8.0 ** -0.5, src=ctxT, src_ready=t_ctxT, bq="l1_bq", bk="l1_bk",
                       bv="l1_bv"),
            "l2": dict(i=2, hd=16, scale=0.25, src=ctxT, src_ready=t_ctxT, bq="l2_bq", bk="l2_bk", bv="l2_bv"),
        }

        def small_keys(name):
            yield from room((work, 2))
            L = LAYERS[name]
            kT, toks = kT_small[L["i"] % 2], []
            kT_free = [pool.now()]
            for o in range(DC):
                bank, free, i = work.take()
                w = w_small[f"{name}_wk"]
                tok = pe.run([step(nc.tensor.matmul,
                    bank[:, :], w[:, c, o * P:(o + 1) * P], L["src"][:, c, :], start=(c == 0), stop=(c == DC - 1))
                    for c in range(DC)], *free, *L["src_ready"], loads[f"{name}_wk"])
                if L["bk"]:
                    t = act.do(step(nc.scalar.activation, kT[:, o, :], bank[:, :], ACT.Identity,
                                                                      bias=col(L["bk"], o)), tok, *kT_free, loads["cols"])
                else:
                    t = act.do(step(nc.scalar.activation, kT[:, o, :], bank[:, :], ACT.Copy), tok, *kT_free)
                toks.append(t)
                work.release(i, t)
            L["kT_ready"] = toks
            yield []

        def small_attention(name, b):
            L = LAYERS[name]
            hd, w = L["hd"], {k: w_small[f"{name}_w{k}"] for k in "qvo"}
            heads = D // hd
            chunk_heads = P // hd
            pairs, vw = heads // 2, 2 * hd + 2
            xb = x[:, TT * b:TT * (b + 1), :]

            yield from room((kdiag, 1), (vdiag[hd], 1), (work, 1))
            kd, kd_free, i_kd = kdiag.take()
            kT = kT_small[L["i"] % 2]
            for c in range(DC):
                t_kd = pool.do(step(nc.gpsimd.tensor_tensor,
                    kd[:, c, 0:chunk_heads * S].rearrange("p (h s) -> p h s", s=S),
                    kT[:, c, b * S:(b + 1) * S].unsqueeze(1).broadcast_to([P, chunk_heads, S]),
                    head_of_row[hd].unsqueeze(2).broadcast_to([P, chunk_heads, S]), ALU.mult),
                    *kd_free, *L["kT_ready"], loads["maskhead"], loads["maskhead8"])

            bank, free, i = work.take()
            tok = pe.run([step(nc.tensor.matmul,
                bank[j * S:(j + 1) * S, 0:D], L["src"][:, c, b * S:(b + 1) * S], w["v"][:, c, :],
                start=(c == 0), stop=(c == DC - 1), skip_group_check=True)
                for c in range(DC) for j in range(2)], *free, *L["src_ready"], loads[f"{name}_wv"])
            vd, vd_free, i_vd = vdiag[hd].take()
            t_vd = []
            for j in range(2):
                src = bank[j * S:(j + 1) * S, 0:D].rearrange("p (q j d) -> p q j d", j=2, d=hd)[:, :, j, :]
                dst = vd[j * S:(j + 1) * S, :, j * hd:(j + 1) * hd]
                if L["bv"]:
                    bias = row(L["bv"])[j * S:(j + 1) * S, :].rearrange("p (q j d) -> p q j d", j=2, d=hd)[:, :, j, :]
                    t_vd.append(dve.do(step(nc.vector.tensor_tensor, dst, src, bias, ALU.add),
                                       tok, *vd_free, loads["rows_early"]))
                else:
                    t_vd.append(dve.do(step(nc.vector.tensor_copy, dst, src), tok, *vd_free))
            work.release(i, *t_vd)
            yield x_ready[b]
            yield from room((norm_ring, 1), (stat, 1))

            after = x_ready[b]
            if name == "l2":
                st, st_free, i_st = stat.take()
                xn, xn_free, i_xn = norm_ring.take()
                t_x = yield from normalise(xb, xn, 1e-5, st, [*after, *st_free, *xn_free], TT)
                stat.release(i_st, t_x)
                yield first([t_x])
                yield from room((work, 1), (srcT_ring, 1))
                bank, tok, i = transpose_tiles(xn, [t_x])
                norm_ring.release(i_xn, tok)
            else:
                yield from room((work, 1), (srcT_ring, 1))
                bank, tok, i = transpose_tiles(xb, after)
                t_x = tok
            sT, sT_free, i_sT = srcT_ring.take()
            t_sT = affine_evac(bank, tok, i, sT, sT_free, *(("l2_g1", "l2_b1") if name == "l2" else ()))
            if name != "l0":
                t_xb = pool.do(step(nc.gpsimd.tensor_tensor,
                    xb, xb, row(f"{name}_bo").unsqueeze(1).broadcast_to([P, TT, D]), ALU.add),
                    *after, t_x, loads["rows_early"], loads["rows_late"])
            else:
                t_xb = None
            yield [t_sT]

            yield from room((work, 1), (qT_ring, 1))
            bank, free, i = work.take()
            tok = pe.run([step(nc.tensor.matmul,
                bank[:, o * T:(o + 1) * T], w["q"][:, c, o * P:(o + 1) * P], sT[:, c, :], start=(c == 0),
                stop=(c == DC - 1)) for o in range(DC) for c in range(DC)], *free, t_sT, loads[f"{name}_wq"])
            srcT_ring.release(i_sT, tok)
            qT, qT_free, i_qT = qT_ring.take()
            t_qT = affine_evac(bank, tok, i, qT, qT_free, None, L["bq"])
            yield [t_qT, t_kd]

            yield from room((o_ring, 1))
            o_buf, o_free, i_o = o_ring.take()
            t_o = []
            for t in range(TT):
                for g in range(heads // GH):
                    yield from room((score_ring, 1), (probs, 1), (stat, 1))
                    sc, sc_free, i_sc = score_ring.take()
                    parts = []
                    for half in range(2):
                        c, k0 = (half, 0) if chunk_heads == 8 else (g, half * BANK)
                        parts.append(step(nc.tensor.matmul,
                            sc[:, half * BANK:(half + 1) * BANK], qT[:, c, t * P:(t + 1) * P],
                            kd[:, c, k0:k0 + BANK], start=True, stop=(name == "l1")))
                        if name != "l1":
                            parts.append(step(nc.tensor.matmul,
                                sc[:, half * BANK:(half + 1) * BANK], ones_row[:, :],
                                mask_row[name][:, b * S:(b + 1) * S].unsqueeze(1).broadcast_to([1, 8, S]),
                                start=False, stop=True))
                    tok = pe.run(parts, *sc_free, t_qT, t_kd, t_ones_row, t_inf)
                    yield first([tok])
                    st, st_free, i_st = stat.take()
                    pr, pr_free, i_pr = probs.take()
                    e3 = pr[:, 0:GS].rearrange("p (h s) -> p h s", s=S)
                    s3 = sc[:, :].rearrange("p (h s) -> p h s", s=S)
                    bmax = st[:, 0:GH].unsqueeze(2).broadcast_to([P, GH, S])
                    if name == "l1":
                        msk = mask_tok[:, TT * b + t, :].unsqueeze(1).broadcast_to([P, GH, S])
                        t0 = dve.do(step(nc.vector.scalar_tensor_tensor, out=e3, in0=s3, scalar=L["scale"], in1=msk,
                                                                     op0=ALU.mult, op1=ALU.add),
                                    tok, *pr_free, loads["mask_tok"])
                        score_ring.release(i_sc, t0)
                        t1 = dve.do(step(nc.vector.tensor_reduce, st[:, 0:GH], e3, X, ALU.max), t0, *st_free)
                        t2 = dve.do(step(nc.vector.tensor_tensor, e3, e3, bmax, ALU.subtract), t1)
                    else:
                        t1 = dve.do(step(nc.vector.tensor_reduce, st[:, 0:GH], s3, X, ALU.max), tok, *st_free)
                        t2 = dve.do(step(nc.vector.tensor_tensor, e3, s3, bmax, ALU.subtract), t1, *pr_free)
                        score_ring.release(i_sc, t2)
                    stat.release(i_st, t2)
                    yield first([t2])
                    scale = 1.0 if name == "l1" else L["scale"]
                    t_e = act.do(step(nc.scalar.activation, pr[:, 0:GS], pr[:, 0:GS], ACT.Exp, scale=scale), t2)
                    yield [t_e]

                    yield from room((probsT, 1), (work, 2))
                    pT, pT_free, i_pT = probsT.take()
                    t_pT = []
                    for half in range(2):
                        bank, free, i = work.take()
                        tok = pe.run([step(nc.tensor.transpose,
                            bank[:, q * P:(q + 1) * P], pr[:, (4 * half + q) * P:(4 * half + q + 1) * P],
                            ident[:, :]) for q in range(4)], *free, t_e)
                        dst = pT[:, 4 * half:4 * half + 4, :].rearrange("p q t -> p (q t)")
                        t2 = act.do(step(nc.scalar.activation, dst, bank[:, :], ACT.Copy), tok, *pT_free)
                        t_pT.append(t2)
                        work.release(i, t2)
                    probs.release(i_pr, tok)
                    yield t_pT

                    yield from room((work, 1), (stat, 1))
                    bank, free, i = work.take()
                    tok = pe.run([step(nc.tensor.matmul,
                        bank[:, q * vw:(q + 1) * vw], pT[:, q, :], vd[:, 8 * g + q, :], start=True, stop=True)
                        for q in range(8)], *free, *t_pT, *t_vd)
                    probsT.release(i_pT, tok)
                    yield first([tok])
                    st, st_free, i_st = stat.take()
                    b3 = bank[:, 0:8 * vw].rearrange("p (q w) -> p q w", w=vw)
                    t0 = dve.do(step(nc.vector.reciprocal, st[:, 0:GH].rearrange("p (q j) -> p q j", j=2),
                                                       b3[:, :, 2 * hd:vw]), tok, *st_free)
                    t1 = dve.do(step(nc.vector.tensor_tensor,
                        o_buf[:, t, g * GH * hd:(g + 1) * GH * hd].rearrange("p (q j d) -> p q j d", j=2, d=hd),
                        b3[:, :, 0:2 * hd].rearrange("p q (j d) -> p q j d", j=2),
                        st[:, 0:GH].rearrange("p (q j) -> p q j", j=2).unsqueeze(3).broadcast_to([P, 8, 2, hd]),
                        ALU.mult), t0, *o_free)
                    work.release(i, t1)
                    stat.release(i_st, t1)
                    t_o.append(t1)
                    yield [t1] if t == TT - 1 and g == heads // GH - 1 else []
            qT_ring.release(i_qT, pe.now())
            kdiag.release(i_kd, pe.now())
            vdiag[hd].release(i_vd, pe.now())

            yield from room((work, 1), (oT_ring, 1))
            bank, tok, i = transpose_tiles(o_buf, t_o)
            o_ring.release(i_o, tok)
            oT, oT_free, i_oT = oT_ring.take()
            t_oT = affine_evac(bank, tok, i, oT, oT_free)
            yield [t_oT]
            yield from room((work, 1))
            bank, free, i = work.take()
            tok = pe.run([step(nc.tensor.matmul,
                bank[:, t * D:(t + 1) * D], oT[:, c, t * P:(t + 1) * P], w["o"][:, c, :], start=(c == 0),
                stop=(c == DC - 1)) for t in range(TT) for c in range(DC)], *free, t_oT, loads[f"{name}_wo"])
            oT_ring.release(i_oT, tok)
            yield first([tok])
            y3 = bank[:, :].rearrange("p (t d) -> p t d", t=TT)
            if name == "l0":
                t_x = dve.do(step(nc.vector.scalar_tensor_tensor, out=xb, in0=y3, scalar=tanh_gate[:, 0:1], in1=xb,
                                                              op0=ALU.mult, op1=ALU.add), tok, t_gate)
                work.release(i, t_x)
            else:
                t_x = dve.do(step(nc.vector.tensor_tensor, xb, y3, xb, ALU.add), tok, t_xb)
                work.release(i, t_x)
            if name == "l1":
                yield from room((stat, 1))
                st, st_free, i_st = stat.take()
                t1 = yield from normalise(xb, xb, 1e-6, st, [t_x, *st_free], TT)
                stat.release(i_st, t1)
                yield first([t1])
                t2 = pool.do(step(nc.gpsimd.tensor_tensor,
                    xb, xb, row("l1_g").unsqueeze(1).broadcast_to([P, TT, D]), ALU.mult), t1)
                t_x = pool.do(step(nc.gpsimd.tensor_tensor,
                    xb, xb, row("l1_b").unsqueeze(1).broadcast_to([P, TT, D]), ALU.add), t2)
            x_ready[b] = [t_x]
            yield []

        def split(whole, parts, *after):
            hi, lo = parts
            t_hi = act.do(step(nc.scalar.activation, hi, whole, ACT.Copy), *after)
            t_lo = dve.do(step(nc.vector.tensor_tensor, lo, whole, hi.bitcast(F32), ALU.subtract), t_hi)
            return [t_hi, t_lo]

        def products(out, stationary, moving, start, stop):
            (s_hi, s_lo), (m_hi, m_lo) = stationary, moving
            pairs = ((s_hi, m_hi), (s_hi, m_lo), (s_lo, m_hi))
            return [step(nc.tensor.matmul, out, a, m, start=start and i == 0, stop=stop and i == 2)
                    for i, (a, m) in enumerate(pairs)]

        def mlp_split(b, w1, w2, ready, gamma, beta, fcb, pb, func, store):
            while not ready:
                yield BLOCKED
            xb = x[:, TT * b:TT * (b + 1), :]
            yield from room((stat, 1), (norm_ring, 1))
            st, st_free, i_st = stat.take()
            xn, xn_free, i_xn = norm_ring.take()
            t_n = yield from normalise(xb, xn, 1e-5, st, [*x_ready[b], *st_free, *xn_free], TT)
            stat.release(i_st, t_n)
            t_xb = pool.do(step(nc.gpsimd.tensor_tensor, xb, xb, row(pb).unsqueeze(1).broadcast_to([P, TT, D]),
                                ALU.add), t_n, loads["rows_late"])
            yield first([t_n])
            yield from room((work, 1), (srcT_ring, 1), (src_parts, 1))
            bank, tok, i = transpose_tiles(xn, [t_n])
            norm_ring.release(i_xn, tok)
            sT, sT_free, i_sT = srcT_ring.take()
            t_sT = affine_evac(bank, tok, i, sT, sT_free, gamma, beta)
            sp_, sp_free, i_sp = src_parts.take()
            t_split = split(sT, sp_, t_sT, *sp_free)
            srcT_ring.release(i_sT, *t_split)
            yield t_split
            yield from room((hid_parts, 1))
            hid, hid_free, i_hid = hid_parts.take()
            t_h = []
            for f in range(0, FC, 2):
                yield from room((work, 1), (hid_whole, 1))
                bank, free, i = work.take()
                tok = pe.run([mm for j in range(2) for c in range(DC) for mm in products(
                    bank[:, j * T:(j + 1) * T], [w[:, c, (f + j) * P:(f + j + 1) * P] for w in w1],
                    [v[:, c, :] for v in sp_], c == 0, c == DC - 1)], *free, *t_split, *ready)
                whole, w_free, i_w = hid_whole.take()
                for j in range(2):
                    t = act.do(step(nc.scalar.activation,
                        whole[:, j, :], bank[:, j * T:(j + 1) * T], func, bias=col(fcb, f + j)), tok, *w_free)
                work.release(i, t)
                t_parts = split(whole, [v[:, f:f + 2, :] for v in hid], t, *hid_free)
                hid_whole.release(i_w, *t_parts)
                t_h += t_parts
                yield []
            src_parts.release(i_sp, tok)
            for t in range(TT):
                if t == 0:
                    yield t_h
                    yield from room((work, 1))
                    bank, free, i = work.take()
                tok = pe.run([mm for f in range(FC) for mm in products(
                    bank[:, t * D:(t + 1) * D], [v[:, f, t * P:(t + 1) * P] for v in hid],
                    [w[:, f, :] for w in w2], f == 0, f == FC - 1)], *free, *t_h)
                yield []
            hid_parts.release(i_hid, tok)
            yield first([tok])
            t_x = dve.do(step(nc.vector.tensor_tensor, xb, bank[:, :].rearrange("p (t d) -> p t d", t=TT), xb,
                              ALU.add), tok, t_xb)
            work.release(i, t_x)
            x_ready[b] = [t_x]
            if store:
                dst = out.rearrange("(n p) d -> p n d", p=P)[:, TT * b:TT * (b + 1), :]
                sp.wait([t_x])
                sp.todo.append(lambda e: e.dma_start(dst, xb).then_inc(s_out, 16))
            yield []

        def mlp(b, w1, w2, ready, gamma, beta, fcb, pb, func, hidden, store):
            xb = x[:, TT * b:TT * (b + 1), :]
            yield from room((stat, 1), (norm_ring, 1))
            st, st_free, i_st = stat.take()
            xn, xn_free, i_xn = norm_ring.take()
            t_n = yield from normalise(xb, xn, 1e-5, st, [*x_ready[b], *st_free, *xn_free], TT)
            stat.release(i_st, t_n)
            t_xb = pool.do(step(nc.gpsimd.tensor_tensor, xb, xb, row(pb).unsqueeze(1).broadcast_to([P, TT, D]),
                                                     ALU.add), t_n, loads["rows_late"])
            yield first([t_n])
            yield from room((work, 1), (srcT_ring, 1))
            bank, tok, i = transpose_tiles(xn, [t_n])
            norm_ring.release(i_xn, tok)
            sT, sT_free, i_sT = srcT_ring.take()
            t_sT = affine_evac(bank, tok, i, sT, sT_free, gamma, beta)
            yield [t_sT]
            yield from room((hidden, 1))
            hid, hid_free, i_hid = hidden.take()
            t_h = []
            for f in range(0, FC, 2):
                yield from room((work, 1))
                bank, free, i = work.take()
                tok = pe.run([step(nc.tensor.matmul,
                    bank[:, j * T:(j + 1) * T], w1[:, c, (f + j) * P:(f + j + 1) * P], sT[:, c, :],
                    start=(c == 0), stop=(c == DC - 1)) for j in range(2) for c in range(DC)],
                    *free, t_sT, *ready)
                for j in range(2):
                    t = act.do(step(nc.scalar.activation,
                        hid[:, f + j, :], bank[:, j * T:(j + 1) * T], func, bias=col(fcb, f + j)), tok, *hid_free)
                t_h.append(t)
                work.release(i, t)
                yield []
            srcT_ring.release(i_sT, tok)
            yield t_h
            yield from room((work, 1))
            bank, free, i = work.take()
            tok = pe.run([step(nc.tensor.matmul,
                bank[:, t * D:(t + 1) * D], hid[:, f, t * P:(t + 1) * P], w2[:, f, :], start=(f == 0),
                stop=(f == FC - 1)) for t in range(TT) for f in range(FC)], *free, *t_h)
            hidden.release(i_hid, tok)
            yield first([tok])
            t_x = dve.do(step(nc.vector.tensor_tensor, xb, bank[:, :].rearrange("p (t d) -> p t d", t=TT), xb,
                                                   ALU.add), tok, t_xb)
            work.release(i, t_x)
            x_ready[b] = [t_x]
            if store:
                dst = out.rearrange("(n p) d -> p n d", p=P)[:, TT * b:TT * (b + 1), :]
                sp.wait([t_x])
                sp.todo.append(lambda e: e.dma_start(dst, xb).then_inc(s_out, 16))
            yield []

        WN = H3 * D
        w3_wq = w3[:, 0:WN].rearrange("p (h d) -> p h d", h=H3)
        w3_wk = w3[:, WN:2 * WN].rearrange("p (c n) -> p c n", c=DC)
        w3_wv = w3[:, 2 * WN:3 * WN].rearrange("p (c n) -> p c n", c=DC)
        w3_wo = w3[:, 3 * WN:4 * WN].rearrange("p (h d) -> p h d", h=H3)
        SCALE3 = float(K3) ** -0.5
        n_kq, n_vo = DC * GS, GH // 2 * D
        pk = [p[:, 0:2 * n_kq].rearrange("p (b c n) -> p b c n", b=2, c=DC) for p in pair]
        pv = [p[:, 2 * n_kq:2 * (n_kq + n_vo)].rearrange("p (b q d) -> p b q d", b=2, q=GH // 2) for p in pair]
        pc = [p[:, 2 * (n_kq + n_vo):].rearrange("p (b n) -> p b n", b=2) for p in pair]
        PAIRS = B // 2
        pair_users, keys_ready, values_ready = {}, {}, {}
        bias_ready = {}

        def load_w3(a, g, which, *after):
            heads = slice(4 * g, 4 * g + 4)
            ks = slice(4 * g * K3, (4 * g + 4) * K3)
            for k, dst, at in (("k", w3_wk, ks), ("q", w3_wq, heads), ("v", w3_wv, ks), ("o", w3_wo, heads)):
                if k not in which:
                    continue
                src = A[f"l3_w{k}{a}"]
                if k in "kv":
                    load(f"l3_w{k}{a}_{g}", dst[:, :, at], src.rearrange("p (c n) -> p c n", c=DC)[:, :, at], *after)
                else:
                    load(f"l3_w{k}{a}_{g}", dst[:, at, :], src.rearrange("p (h d) -> p h d", h=H3)[:, at, :], *after)

        def l3_bias(a):
            yield from room((work, 1))
            bank, free, i = work.take()
            tok = pe.run([step(nc.tensor.matmul, bank[:, 0:D], col(f"l3_vb{a}", h).broadcast_to([P, P]),
                               w3_wo[:, h, :], start=(h == 0), stop=(h == H3 - 1)) for h in range(H3)],
                         *free, *(loads[f"l3_wo{a}_{g}"] for g in range(H3 // 4)), loads["cols"])
            t = dve.do(step(nc.vector.tensor_tensor, row(f"l3_bo{a}"), bank[:, 0:D], row(f"l3_bo{a}"), ALU.add),
                       tok, loads["rows_late"])
            work.release(i, t)
            bias_ready[a] = t
            yield []

        def project_context(w, bias, hs, p, ready):
            yield [ready]
            yield from room((work, 1), (kvT, 1))
            bank, free, i = work.take()
            tok = pe.run([step(nc.tensor.matmul,
                bank[:, h * P:(h + 1) * P], w[:, c, (hs + h) * K3:(hs + h + 1) * K3],
                ctxT[:, c, p * P:(p + 1) * P], start=(c == 0), stop=(c == DC - 1))
                for h in range(4) for c in range(DC)], *free, ready)
            dst, d_free, i_d = kvT.take()
            t = dve.do(step(nc.vector.tensor_tensor,
                dst[:, :, :], bank[:, :].rearrange("p (h s) -> p h s", h=4),
                col(bias, hs, 4).unsqueeze(2).broadcast_to([P, 4, P]), ALU.add), tok, t_differences, *d_free)
            work.release(i, t)
            return dst, t, i_d

        def slot_free(n):
            while len(pair_users.get(n - 2, ())) < 2:
                yield BLOCKED
            return [t for user in pair_users[n - 2] for t in user]

        def l3_keys(a, p):
            n = PAIRS * (a - 1) + p
            s = n % 2
            free_pair = yield from slot_free(n)
            for g in range(H3 // 4):
                hs = 4 * g
                kt, t_kt, i_kt = yield from project_context(w3_wk, f"l3_bk{a}", hs, p, loads[f"l3_wk{a}_{g}"])
                yield [t_kt, loads[f"l3_wq{a}_{g}"]]
                for c in range(DC):
                    yield from room((work, 1))
                    bank, free, i = work.take()
                    tok = pe.run([step(nc.tensor.matmul,
                        bank[:, h * P:(h + 1) * P], w3_wq[:, hs + h, c * P:(c + 1) * P], kt[:, h, :], start=True,
                        stop=True) for h in range(4)], *free, t_kt, loads[f"l3_wq{a}_{g}"])
                    t = act.do(step(nc.scalar.activation,
                        pk[s][:, :, c, hs * S:(hs + 4) * S].rearrange("p b (h k) -> p b h k", h=4),
                        bank[:, :].rearrange("p (h b k) -> p b h k", h=4, b=2), ACT.Copy), tok, *free_pair)
                    work.release(i, t)
                    yield []
                if a == 1 and p == PAIRS - 1:
                    load_w3(2, g, "kq", tok)
                yield from room((work, 1))
                bank, free, i = work.take()
                tok = pe.run([step(nc.tensor.matmul,
                    bank[:, h * P:(h + 1) * P], col(f"l3_bq{a}", hs + h).broadcast_to([P, P]), kt[:, h, :],
                    start=True, stop=True) for h in range(4)], *free)
                t = act.do(step(nc.scalar.activation,
                    pc[s][:, :, hs * S:(hs + 4) * S].rearrange("p b (h k) -> p b h k", h=4),
                    bank[:, :].rearrange("p (h b k) -> p b h k", h=4, b=2), ACT.Copy), tok, *free_pair)
                work.release(i, t)
                kvT.release(i_kt, tok)
                yield []
            keys_ready[n] = t

        def l3_values(a, p):
            n = PAIRS * (a - 1) + p
            s = n % 2
            free_pair = yield from slot_free(n)
            for g in range(H3 // 4):
                hs = 4 * g
                vt, t_vt, i_vt = yield from project_context(w3_wv, f"l3_bv{a}", hs, p, loads[f"l3_wv{a}_{g}"])
                yield [t_vt, loads[f"l3_wo{a}_{g}"]]
                for q in range(2):
                    yield from room((work, 1))
                    bank, free, i = work.take()
                    tok = pe.run([step(nc.tensor.matmul,
                        bank[j * S:(j + 1) * S, bb * D:(bb + 1) * D], vt[:, 2 * q + j, bb * S:(bb + 1) * S],
                        w3_wo[:, hs + 2 * q + j, :], start=True, stop=True, skip_group_check=True)
                        for bb in range(2) for j in range(2)], *free, t_vt, loads[f"l3_wo{a}_{g}"])
                    t = dve.do(step(nc.vector.tensor_copy,
                        pv[s][:, :, hs // 2 + q, :], bank[:, :].rearrange("p (b d) -> p b d", b=2)),
                        tok, *free_pair)
                    work.release(i, t)
                    yield []
                if a == 1 and p == PAIRS - 1:
                    load_w3(2, g, "vo", tok)
                kvT.release(i_vt, tok)
            values_ready[n] = t

        attentions = {}

        def l3_input(a, b):
            while a not in bias_ready:
                yield BLOCKED
            xb = x[:, TT * b:TT * (b + 1), :]
            yield from room((stat, 1), (norm_ring, 1))
            st, st_free, i_st = stat.take()
            xn, xn_free, i_xn = norm_ring.take()
            t_n = yield from normalise(xb, xn, 1e-5, st, [*x_ready[b], *st_free, *xn_free], TT)
            stat.release(i_st, t_n)
            t_xb = pool.do(step(nc.gpsimd.tensor_tensor,
                xb, xb, row(f"l3_bo{a}").unsqueeze(1).broadcast_to([P, TT, D]), ALU.add), t_n,
                bias_ready[a])
            yield first([t_n])
            yield from room((work, 1), (srcT_ring, 1))
            bank, tok, i = transpose_tiles(xn, [t_n])
            norm_ring.release(i_xn, tok)
            sT, sT_free, i_sT = srcT_ring.take()
            t_sT = affine_evac(bank, tok, i, sT, sT_free, f"l3_g{a}", f"l3_b{a}")
            attentions[a, b] = dict(sT=sT, i_sT=i_sT, t_sT=t_sT, t_xb=t_xb, t_x=[], readers=[])
            yield []

        def l3_attention(a, b, t):
            p, bb = divmod(b, 2)
            n = PAIRS * (a - 1) + p
            s = n % 2
            while (a, b) not in attentions or n not in keys_ready:
                yield BLOCKED
            batch = attentions[a, b]
            sT, xb = batch["sT"], x[:, TT * b:TT * (b + 1), :]
            yield [batch["t_sT"]]
            yield from room((score_ring, 1), (probs, 1), (stat, 1))
            sc, sc_free, i_sc = score_ring.take()
            tok = pe.run([step(nc.tensor.matmul,
                sc[:, half * BANK:(half + 1) * BANK], sT[:, c, t * P:(t + 1) * P],
                pk[s][:, bb, c, half * BANK:(half + 1) * BANK], start=(c == 0), stop=(c == DC - 1))
                for half in range(2) for c in range(DC)], *sc_free, batch["t_sT"], keys_ready[n])
            yield first([tok])
            pr, pr_free, i_pr = probs.take()
            st, st_free, i_st = stat.take()
            e3 = pr[:, 0:GS].rearrange("p (h s) -> p h s", s=S)
            eb = pr[:, GS:GS + H3]
            m, den, r = st[:, 0:H3], st[:, 16:32], st[:, 32:48]

            def over_keys(v):
                return v.unsqueeze(2).broadcast_to([P, H3, S])
            t0 = dve.do(step(nc.vector.tensor_tensor, pr[:, 0:GS], sc[:, :], pc[s][:, bb, :], ALU.add), tok,
                        *pr_free)
            score_ring.release(i_sc, t0)
            t1 = dve.do(step(nc.vector.tensor_reduce, m, e3, X, ALU.max), t0, *st_free)
            t1 = dve.do(step(nc.vector.tensor_scalar, m, m, 0.0, None, ALU.max), t1)
            t2 = dve.do(step(nc.vector.tensor_tensor, e3, e3, over_keys(m), ALU.subtract), t1)
            t3 = dve.do(step(nc.vector.tensor_scalar, eb, m, -1.0, None, ALU.mult), t1)
            yield first([t2])
            t_e = act.do(step(nc.scalar.activation, pr[:, :], pr[:, :], ACT.Exp, scale=SCALE3), t2, t3)
            yield first([t_e])
            t4 = dve.do(step(nc.vector.tensor_reduce, den, e3, X, ALU.add), t_e)
            t5 = dve.do(step(nc.vector.tensor_tensor, den, den, eb, ALU.add), t4)
            t6 = dve.do(step(nc.vector.reciprocal, r, den), t5)
            t7 = pool.do(step(nc.gpsimd.tensor_tensor, e3, e3, over_keys(r), ALU.mult), t6)
            stat.release(i_st, t7)
            yield [t7]
            yield from room((probsT, 1), (work, 2))
            pT, pT_free, i_pT = probsT.take()
            t_pT = []
            for half in range(2):
                bank, free, i = work.take()
                tok = pe.run([step(nc.tensor.transpose,
                    bank[:, q * P:(q + 1) * P], pr[:, (4 * half + q) * P:(4 * half + q + 1) * P],
                    ident[:, :]) for q in range(4)], *free, t7)
                dst = pT[:, 4 * half:4 * half + 4, :].rearrange("p q t -> p (q t)")
                t2 = act.do(step(nc.scalar.activation, dst, bank[:, :], ACT.Copy), tok, *pT_free)
                t_pT.append(t2)
                work.release(i, t2)
            probs.release(i_pr, tok)
            while n not in values_ready:
                yield BLOCKED
            yield t_pT
            yield from room((work, 1))
            bank, free, i = work.take()
            tok = pe.run([step(nc.tensor.matmul, bank[:, 0:D], pT[:, q, :], pv[s][:, bb, q, :],
                               start=(q == 0), stop=(q == GH // 2 - 1)) for q in range(GH // 2)],
                         *free, *t_pT, values_ready[n])
            probsT.release(i_pT, tok)
            yield first([tok])
            t_x = dve.do(step(nc.vector.tensor_tensor, xb[:, t, :], bank[:, 0:D], xb[:, t, :], ALU.add),
                         tok, batch["t_xb"])
            work.release(i, t_x)
            batch["t_x"].append(t_x)
            batch["readers"] += [tok, t0]
            if len(batch["t_x"]) == TT:
                srcT_ring.release(batch["i_sT"], pe.now())
                x_ready[b] = batch["t_x"]
                pair_users.setdefault(n, []).append(batch["readers"])
            yield []

        s_out = sem("s_out")

        small = [small_keys("l0")]
        for name in ("l0", "l1", "l2"):
            if name != "l0":
                small.insert(len(small) - 2, small_keys(name))
            small += [small_attention(name, b) for b in range(B)]
        interleave(pe, small, 5)
        w3_free = so_far()
        for g in range(H3 // 4):
            load_w3(1, g, "kqvo", *w3_free)
        hid_l2 = Ring(hid_bufs, w3_free)
        probs, probsT = Ring([*probs_bufs, probs_late[:, :]], w3_free), Ring(probsT_bufs, w3_free)
        pair_users[-2] = [w3_free, []]
        mlps = [mlp(b, *w_mlp["l2"], [loads["l2_fc"], loads["l2_pr"]], "l2_g2", "l2_b2", "l2_fcb", "l2_pb",
                    ACT.Gelu_apprx_tanh, hid_l2, False) for b in range(B)]
        interleave(pe, mlps[:5], 3, young=True)

        def chain(*gens):
            for g in gens:
                yield from g
        interleave(pe, mlps[5:], 3, l3_keys(1, 0), chain(l3_values(1, 0), l3_bias(1)))
        pair_users[-1] = [so_far(), []]
        srcT_ring = Ring([fixed[0], fixed[1]], so_far())
        norm_ring = Ring([fixed[2], fixed[3]], so_far())

        def parts_at(name, offset, *shape):
            n = 4
            for k in shape:
                n *= k
            both = [nc.alloc_sbuf_tensor_at(f"{name}_{k}", [P, *shape], F32R, offset=offset + i * n)[:, :, :]
                    for i, k in enumerate(("high", "low"))]
            return both, offset + 2 * n

        raw = w3[:, 0:2 * DC * F].rearrange("p (w n) -> p w n", w=2)
        w1_parts, at = parts_at("w1", pair_at[0], DC, F)
        w2_parts, at = parts_at("w2", at, FC, D)
        src_bufs, hid_parts_bufs = [], []
        for i in range(2):
            both, at = parts_at(f"src{i}", at, DC, T)
            src_bufs.append(both)
        at = w3_at + 4 * 2 * DC * F
        for i in range(2):
            both, at = parts_at(f"hid{i}", at, FC, T)
            hid_parts_bufs.append(both)
        cut = carve(w3[:, 6 * DC * F:])
        hid_whole_bufs = [cut(2, T) for _ in range(4)]
        weights_split = []

        def mlp_weights():
            nonlocal w3_free, src_parts, hid_parts, hid_whole
            w3_free = so_far()
            load("l3_fc", raw[:, 0, :], A["l3_fc"], *w3_free)
            load("l3_pr", raw[:, 1, :], A["l3_pr"], *w3_free)
            free_pair = yield from slot_free(2 * PAIRS)
            while 2 * PAIRS - 1 not in values_ready:
                yield BLOCKED
            w3_free = so_far()
            src_parts, hid_parts = Ring(src_bufs, free_pair), Ring(hid_parts_bufs, w3_free)
            hid_whole = Ring(hid_whole_bufs, w3_free)
            tokens = []
            for w, both, name in ((0, w1_parts, "l3_fc"), (1, w2_parts, "l3_pr")):
                n = raw.shape[2] // 4
                flat = [v.rearrange("p a b -> p (a b)") for v in both]
                for k in range(4):
                    yield first([loads[name]])
                    tokens += split(raw[:, w, k * n:(k + 1) * n], [v[:, k * n:(k + 1) * n] for v in flat],
                                    loads[name], *free_pair)
            weights_split.extend(tokens[-2:])
            yield []

        src_parts = hid_parts = hid_whole = None
        streams = [g for a in (1, 2) for b in range(B)
                   for g in (l3_input(a, b), *(l3_attention(a, b, t) for t in range(TT)))]
        streams += [mlp_split(b, w1_parts, w2_parts, weights_split, "l3_gm", "l3_bm", "l3_fcb",
                              "l3_pb", ACT.Gelu, True) for b in range(B)]
        keys = [l3_keys(a, p) for a in (1, 2) for p in range(PAIRS)]
        values = [l3_values(a, p) for a in (1, 2) for p in range(PAIRS)]
        interleave(pe, streams, 5, chain(*keys[1:], mlp_weights()),
                   chain(*values[1:PAIRS + 1], l3_bias(2), *values[PAIRS + 1:]))

        with nc.Block() as block:
            @block.sync
            def _(e):
                sp.emit(e)
                e.wait_ge(s_out, 16 * B)

            @block.tensor
            def _(e):
                pe.emit(e)

            @block.vector
            def _(e):
                dve.emit(e)

            @block.scalar
            def _(e):
                act.emit(e)

            @block.gpsimd
            def _(e):
                pool.emit(e)


def kernel(**inputs):
    import numpy as np
    import concourse.bacc as bacc
    from concourse.bass_utils import run_bass_kernel_spmd

    v = {k: np.asarray(a) for k, a in inputs.items()}

    def rows_first(w):
        return np.ascontiguousarray(w.reshape(-1, P, w.shape[1]).transpose(1, 0, 2).reshape(P, -1))

    def per_group(w):
        w = w.reshape(-1, 8, 1, 8)
        return np.broadcast_to(w, (w.shape[0], 8, 4, 8)).reshape(w.shape[0], D)

    a = {"x": v["x"].reshape(B * T, D), "ctx": v["ctx_2048"].reshape(CTX, D),
         "mask": v["mask_BxS2_bf1"].view(np.uint8).reshape(1, CTX),
         "mask_tok": v["mask_Bx1xSxS2_ff0"].reshape(B * T, S)}
    for n, w in (("q", "Wq"), ("k", "Wk"), ("v", "Wv"), ("o", "Wo")):
        a[f"l0_w{n}"] = rows_first(v[f"L0_xattn_{w}"].T)
        m = v[f"L1_xattn_{w}"]
        a[f"l1_w{n}"] = rows_first(per_group(m) if n in "kv" else m)
        a[f"l2_w{n}"] = rows_first(v["L2_xattn_cproj_w" if n == "o" else f"L2_xattn_{n}_w"])
    a["l2_fc"], a["l2_pr"] = rows_first(v["L2_xattn_fc_w"]), rows_first(v["L2_xattn_proj_w"])
    a["l3_fc"], a["l3_pr"] = rows_first(v["L3_xattn_w_fc1"]), rows_first(v["L3_xattn_w_fc2"])
    for i in "12":
        a[f"l3_wq{i}"] = rows_first(v[f"L3_xattn_wq{i}"].T)
        for n in "kvo":
            a[f"l3_w{n}{i}"] = rows_first(v[f"L3_xattn_w{n}{i}"])
    named = {"l0_g": "L0_xattn_ln_gamma", "l0_b": "L0_xattn_ln_beta", "l1_bq": "L1_xattn_bq",
             "l2_g1": "L2_xattn_ln1_w", "l2_b1": "L2_xattn_ln1_b", "l2_bq": "L2_xattn_q_b", "l2_bk": "L2_xattn_k_b",
             "l2_g2": "L2_xattn_ln2_w", "l2_b2": "L2_xattn_ln2_b", "l2_fcb": "L2_xattn_fc_b",
             "l3_gm": "L3_xattn_ln_mlp_scale", "l3_bm": "L3_xattn_ln_mlp_offset", "l3_fcb": "L3_xattn_b_fc1"}
    for i in "12":
        named |= {f"l3_g{i}": f"L3_xattn_ln{i}_scale", f"l3_b{i}": f"L3_xattn_ln{i}_offset",
                  f"l3_bq{i}": f"L3_xattn_bq{i}", f"l3_bk{i}": f"L3_xattn_bk{i}", f"l3_bv{i}": f"L3_xattn_bv{i}",
                  f"l3_kb{i}": f"L3_xattn_bias_k{i}", f"l3_vb{i}": f"L3_xattn_bias_v{i}"}
    parts = []
    for n in COLS:
        if n == "gate":
            c = np.broadcast_to(v["L0_xattn_gate"].reshape(1, 1), (P, 1))
        elif n == "l1_bk":
            c = per_group(v["L1_xattn_bk"]).reshape(-1, P).T
        else:
            c = v[named[n]].reshape(-1, P).T
        parts.append(c)
    a["cols"] = np.ascontiguousarray(np.concatenate(parts, axis=1))
    rows = {"l1_bv": per_group(v["L1_xattn_bv"]), "l1_bo": v["L1_xattn_bo"], "l1_g": v["L1_xattn_gamma"],
            "l1_b": v["L1_xattn_beta"], "l2_bv": v["L2_xattn_v_b"], "l2_bo": v["L2_xattn_cproj_b"],
            "l2_pb": v["L2_xattn_proj_b"], "l3_bo1": v["L3_xattn_bo1"], "l3_bo2": v["L3_xattn_bo2"],
            "l3_pb": v["L3_xattn_b_fc2"]}
    a["rows"] = np.concatenate([rows[n].reshape(1, D) for n in ROWS], axis=0)
    a["ident"] = np.eye(P, dtype=np.float32)
    for hd in (16, 8):
        a[f"head{hd}"] = (np.arange(P)[:, None] // hd == np.arange(P // hd)[None, :]).astype(np.float32)

    nc = bacc.Bacc("TRN2", target_bir_lowering=False, num_devices=1)
    arrays, args = {}, {}
    for n, arr in a.items():
        arrays[f"in_{n}"] = np.ascontiguousarray(arr)
        args[n] = nc.dram_tensor(f"in_{n}", arr.shape, mybir.dt.from_np(arr.dtype), kind="ExternalInput").ap()
    out = nc.dram_tensor("out", (B * T, D), F32, kind="ExternalOutput").ap()
    build(nc, args, out)
    r = run_bass_kernel_spmd(nc, [arrays], core_ids=[0])
    return r.results[0]["out"].reshape(B, T, D)
```
